# Optimizing a Trainium2 kernel written in Bass

```python
import numpy as np
import jax
import jax.numpy as jnp

def _softmax(x, axis=-1):
    return jax.nn.softmax(x, axis=axis)

def _gelu(x):
    return jax.nn.gelu(x, approximate=True)

def _silu(x):
    return jax.nn.silu(x)

def _sigmoid(x):
    return jax.nn.sigmoid(x)

def _layernorm(x, axis=-1, eps=1e-05):
    m = jnp.mean(x, axis=axis, keepdims=True)
    v = jnp.var(x, axis=axis, keepdims=True)
    return (x - m) / jnp.sqrt(v + eps)

def _scatter_add(tgt, idx, src, axis=0):
    return tgt.at[idx].add(src)

def _segment_sum(src, seg, n):
    return jax.ops.segment_sum(src, seg, n)
kernel_name = 'mk_gnn_preln_d4_gnn_r16_f115ff'

def setup_inputs(seed: int=0):
    np.random.seed(seed)
    _w = jnp.asarray

    def _rec_inputs():
        import jax
        import jax.numpy as jnp
        _gk = jax.random.key(seed)
        x = -0.0003713 + 1 * jax.random.normal(jax.random.fold_in(_gk, 1), (3125, 256), jnp.float32)
        _s = jax.random.randint(jax.random.fold_in(_gk, 2), (50000,), 0, 3125, jnp.int32)
        _d = jax.random.randint(jax.random.fold_in(_gk, 3), (50000,), 0, 3125, jnp.int32)
        _loop = jnp.arange(3125, dtype=jnp.int32)
        src = jnp.concatenate([_s, _d, _loop])
        dst = jnp.concatenate([_d, _s, _loop])
        _o = jnp.argsort(dst, stable=True)
        src = src[_o]
        dst = dst[_o]
        edge_attr_20 = jax.random.uniform(jax.random.fold_in(_gk, 12), (103125, 20), jnp.float32, 0.0, 1)
        edge_weight = jax.random.uniform(jax.random.fold_in(_gk, 14), (103125,), jnp.float32, 0.0, 0.999998)
        edge_weight_n2 = jax.random.uniform(jax.random.fold_in(_gk, 15), (103125,), jnp.float32, 0.0, 0.999998)
        return (x, src, dst, edge_attr_20, edge_weight, edge_weight_n2)
    x, src, dst, edge_attr_20, edge_weight, edge_weight_n2 = _rec_inputs()

    def _L0_gnn_setup():
        import jax, jax.numpy as jnp
        import numpy as np
        N_NODES = 3125
        N_EDGES = 50000
        IN_DIM = 256
        HEADS = 4
        F_HEAD = 64
        NEG_SLOPE = 0.2
        key = jax.random.key(seed)
        k1, k2, k3, k4, k5 = jax.random.split(key, 5)
        x = jax.random.normal(k1, (N_NODES, IN_DIM), dtype=jnp.float32)
        edge_index = jax.random.randint(k2, (2, N_EDGES), 0, N_NODES, dtype=jnp.int64)
        scale = 1.0 / np.sqrt(IN_DIM)
        W = jax.random.normal(k3, (HEADS, IN_DIM, F_HEAD), dtype=jnp.float32) * scale
        att_src = jax.random.normal(k4, (HEADS, F_HEAD), dtype=jnp.float32) * scale
        att_dst = jax.random.normal(k5, (HEADS, F_HEAD), dtype=jnp.float32) * scale
        bias = jnp.zeros((HEADS * F_HEAD,), dtype=jnp.float32)
        return {'x': x, 'edge_index': edge_index, 'W': W, 'att_src': att_src, 'att_dst': att_dst, 'bias': bias}
    _L0_gnn_all = _L0_gnn_setup()
    _L0_gnn_in = {k: v for k, v in _L0_gnn_all.items() if k in ('W', 'att_src', 'att_dst', 'bias')}
    del _L0_gnn_all

    def _L1_gnn_setup():
        import jax, jax.numpy as jnp
        import numpy as np
        N, E, HDIM, NG = (625, 20000, 256, 20)
        BN_EPS = 1e-05
        key = jax.random.key(seed)
        ks = jax.random.split(key, 12)
        inp = {'x': jax.random.normal(ks[0], (N, HDIM), dtype=jnp.float32), 'rbf': jax.random.uniform(ks[1], (E, NG), dtype=jnp.float32), 'ei': jax.random.randint(ks[2], (2, E), 0, N, dtype=jnp.int64), 'Wf1': jax.random.normal(ks[3], (NG, HDIM), dtype=jnp.float32) / np.sqrt(NG), 'bf1': jnp.zeros((HDIM,), dtype=jnp.float32), 'Wf2': jax.random.normal(ks[4], (HDIM, HDIM), dtype=jnp.float32) / np.sqrt(HDIM), 'bf2': jnp.zeros((HDIM,), dtype=jnp.float32), 'Wu1': jax.random.normal(ks[5], (HDIM, HDIM), dtype=jnp.float32) / np.sqrt(HDIM), 'bu1': jnp.zeros((HDIM,), dtype=jnp.float32), 'Wu2': jax.random.normal(ks[6], (HDIM, HDIM), dtype=jnp.float32) / np.sqrt(HDIM), 'bu2': jnp.zeros((HDIM,), dtype=jnp.float32), 'gamma': jnp.ones((HDIM,), dtype=jnp.float32), 'beta': jnp.zeros((HDIM,), dtype=jnp.float32)}
        return inp
    _L1_gnn_all = _L1_gnn_setup()
    _L1_gnn_in = {k: v for k, v in _L1_gnn_all.items() if k in ('Wf1', 'bf1', 'Wf2', 'bf2', 'Wu1', 'bu1', 'Wu2', 'bu2', 'gamma', 'beta')}
    del _L1_gnn_all

    def _L2_gnn_setup():
        import jax, jax.numpy as jnp
        import numpy as np
        N_NODES = 6250
        N_EDGES = 50000
        DIM = 256
        EPS = 1e-05
        key = jax.random.key(seed)
        ks = jax.random.split(key, 12)
        H = DIM
        s = 1.0 / np.sqrt(H)
        s2 = 1.0 / np.sqrt(2 * H)
        return {'feat': jax.random.normal(ks[0], (N_NODES, DIM), dtype=jnp.float32), 'src': jax.random.randint(ks[1], (N_EDGES,), 0, N_NODES, dtype=jnp.int32), 'dst': jax.random.randint(ks[2], (N_EDGES,), 0, N_NODES, dtype=jnp.int32), 'iw': jax.random.uniform(ks[3], (N_EDGES,), dtype=jnp.float32), 'ow': jax.random.uniform(ks[4], (N_EDGES,), dtype=jnp.float32), 'gamma': jnp.ones((DIM,), jnp.float32), 'beta': jnp.zeros((DIM,), jnp.float32), 'W_in': jax.random.uniform(ks[5], (H, H), jnp.float32, -s, s), 'b_in': jax.random.uniform(ks[6], (H,), jnp.float32, -s, s), 'W_out': jax.random.uniform(ks[7], (H, H), jnp.float32, -s, s), 'b_out': jax.random.uniform(ks[8], (H,), jnp.float32, -s, s), 'W_x2i': jax.random.uniform(ks[9], (2 * H, 2 * H), jnp.float32, -s2, s2), 'b_x2i': jax.random.uniform(ks[10], (2 * H,), jnp.float32, -s2, s2), 'W_h2h': jax.random.uniform(ks[11], (H, 2 * H), jnp.float32, -s, s)}
    _L2_gnn_all = _L2_gnn_setup()
    _L2_gnn_in = {k: v for k, v in _L2_gnn_all.items() if k in ('gamma', 'beta', 'W_in', 'b_in', 'W_out', 'b_out', 'W_x2i', 'b_x2i', 'W_h2h')}
    del _L2_gnn_all

    def _L3_gnn_setup():
        import jax, jax.numpy as jnp
        import numpy as np
        N_NODES = 3125
        N_EDGES = 100000
        IN_CH = 256
        LAT = 32
        HID = 64
        OUT_CH = 256
        GAT_H = 32

        def _bn_relu(h, g, b):
            m = jnp.mean(h, axis=0)
            v = jnp.var(h, axis=0)
            return jax.nn.relu((h - m) * jax.lax.rsqrt(v + 1e-05) * g + b)

        def _gat(h_in, src, dst, W, a_s, a_d, b):
            N = h_in.shape[0]
            h = h_in @ W
            e = jax.nn.leaky_relu((h @ a_s)[src] + (h @ a_d)[dst], 0.2)
            m = jax.ops.segment_max(e, dst, num_segments=N)
            ex = jnp.exp(e - m[dst])
            den = jax.ops.segment_sum(ex, dst, num_segments=N)
            alpha = ex / den[dst]
            out = jax.ops.segment_sum(alpha[:, None] * h[src], dst, num_segments=N)
            return out + b
        key = jax.random.key(seed)
        ks = jax.random.split(key, 30)
        nrm = lambda k, shape, s=0.05: jax.random.normal(k, shape, dtype=jnp.float32) * s
        inp = {}
        inp['x'] = jax.random.normal(ks[0], (N_NODES, IN_CH), dtype=jnp.float32)
        inp['edge_index'] = jax.random.randint(ks[1], (2, N_EDGES), 0, N_NODES)
        inp['W_g1'] = nrm(ks[2], (IN_CH, GAT_H))
        inp['as_g1'] = nrm(ks[3], (GAT_H,))
        inp['ad_g1'] = nrm(ks[4], (GAT_H,))
        inp['b_g1'] = jnp.zeros((GAT_H,), jnp.float32)
        inp['W_g2'] = nrm(ks[5], (GAT_H, GAT_H))
        inp['as_g2'] = nrm(ks[6], (GAT_H,))
        inp['ad_g2'] = nrm(ks[7], (GAT_H,))
        inp['b_g2'] = jnp.zeros((GAT_H,), jnp.float32)
        inp['W_gf'] = nrm(ks[8], (GAT_H, LAT))
        inp['b_gf'] = jnp.zeros((LAT,), jnp.float32)
        inp['W_m1'] = nrm(ks[9], (IN_CH, HID))
        inp['b_m1'] = jnp.zeros((HID,), jnp.float32)
        inp['g_m1'] = jnp.ones((HID,), jnp.float32)
        inp['be_m1'] = jnp.zeros((HID,), jnp.float32)
        inp['W_m2'] = nrm(ks[10], (HID, HID))
        inp['b_m2'] = jnp.zeros((HID,), jnp.float32)
        inp['g_m2'] = jnp.ones((HID,), jnp.float32)
        inp['be_m2'] = jnp.zeros((HID,), jnp.float32)
        inp['W_m3'] = nrm(ks[11], (HID, LAT))
        inp['b_m3'] = jnp.zeros((LAT,), jnp.float32)
        inp['g_m3'] = jnp.ones((LAT,), jnp.float32)
        inp['be_m3'] = jnp.zeros((LAT,), jnp.float32)
        inp['W_f'] = nrm(ks[12], (LAT, OUT_CH))
        inp['b_f'] = jnp.zeros((OUT_CH,), jnp.float32)
        return inp
    _L3_gnn_all = _L3_gnn_setup()
    _L3_gnn_in = {k: v for k, v in _L3_gnn_all.items() if k in ('W_g1', 'as_g1', 'ad_g1', 'b_g1', 'W_g2', 'as_g2', 'ad_g2', 'b_g2', 'W_gf', 'b_gf', 'W_m1', 'b_m1', 'g_m1', 'be_m1', 'W_m2', 'b_m2', 'g_m2', 'be_m2', 'W_m3', 'b_m3', 'g_m3', 'be_m3', 'W_f', 'b_f')}
    del _L3_gnn_all
    return {'x': x, 'src': src, 'dst': dst, 'edge_attr_20': edge_attr_20, 'edge_weight': edge_weight, 'edge_weight_n2': edge_weight_n2, 'L0_gnn_W': _L0_gnn_in['W'], 'L0_gnn_att_src': _L0_gnn_in['att_src'], 'L0_gnn_att_dst': _L0_gnn_in['att_dst'], 'L0_gnn_bias': _L0_gnn_in['bias'], 'L1_gnn_Wf1': _L1_gnn_in['Wf1'], 'L1_gnn_bf1': _L1_gnn_in['bf1'], 'L1_gnn_Wf2': _L1_gnn_in['Wf2'], 'L1_gnn_bf2': _L1_gnn_in['bf2'], 'L1_gnn_Wu1': _L1_gnn_in['Wu1'], 'L1_gnn_bu1': _L1_gnn_in['bu1'], 'L1_gnn_Wu2': _L1_gnn_in['Wu2'], 'L1_gnn_bu2': _L1_gnn_in['bu2'], 'L1_gnn_gamma': _L1_gnn_in['gamma'], 'L1_gnn_beta': _L1_gnn_in['beta'], 'L2_gnn_gamma': _L2_gnn_in['gamma'], 'L2_gnn_beta': _L2_gnn_in['beta'], 'L2_gnn_W_in': _L2_gnn_in['W_in'], 'L2_gnn_b_in': _L2_gnn_in['b_in'], 'L2_gnn_W_out': _L2_gnn_in['W_out'], 'L2_gnn_b_out': _L2_gnn_in['b_out'], 'L2_gnn_W_x2i': _L2_gnn_in['W_x2i'], 'L2_gnn_b_x2i': _L2_gnn_in['b_x2i'], 'L2_gnn_W_h2h': _L2_gnn_in['W_h2h'], 'L3_gnn_W_g1': _L3_gnn_in['W_g1'], 'L3_gnn_as_g1': _L3_gnn_in['as_g1'], 'L3_gnn_ad_g1': _L3_gnn_in['ad_g1'], 'L3_gnn_b_g1': _L3_gnn_in['b_g1'], 'L3_gnn_W_g2': _L3_gnn_in['W_g2'], 'L3_gnn_as_g2': _L3_gnn_in['as_g2'], 'L3_gnn_ad_g2': _L3_gnn_in['ad_g2'], 'L3_gnn_b_g2': _L3_gnn_in['b_g2'], 'L3_gnn_W_gf': _L3_gnn_in['W_gf'], 'L3_gnn_b_gf': _L3_gnn_in['b_gf'], 'L3_gnn_W_m1': _L3_gnn_in['W_m1'], 'L3_gnn_b_m1': _L3_gnn_in['b_m1'], 'L3_gnn_g_m1': _L3_gnn_in['g_m1'], 'L3_gnn_be_m1': _L3_gnn_in['be_m1'], 'L3_gnn_W_m2': _L3_gnn_in['W_m2'], 'L3_gnn_b_m2': _L3_gnn_in['b_m2'], 'L3_gnn_g_m2': _L3_gnn_in['g_m2'], 'L3_gnn_be_m2': _L3_gnn_in['be_m2'], 'L3_gnn_W_m3': _L3_gnn_in['W_m3'], 'L3_gnn_b_m3': _L3_gnn_in['b_m3'], 'L3_gnn_g_m3': _L3_gnn_in['g_m3'], 'L3_gnn_be_m3': _L3_gnn_in['be_m3'], 'L3_gnn_W_f': _L3_gnn_in['W_f'], 'L3_gnn_b_f': _L3_gnn_in['b_f']}

def reference(x, src, dst, edge_attr_20, edge_weight, edge_weight_n2, L0_gnn_W, L0_gnn_att_src, L0_gnn_att_dst, L0_gnn_bias, L1_gnn_Wf1, L1_gnn_bf1, L1_gnn_Wf2, L1_gnn_bf2, L1_gnn_Wu1, L1_gnn_bu1, L1_gnn_Wu2, L1_gnn_bu2, L1_gnn_gamma, L1_gnn_beta, L2_gnn_gamma, L2_gnn_beta, L2_gnn_W_in, L2_gnn_b_in, L2_gnn_W_out, L2_gnn_b_out, L2_gnn_W_x2i, L2_gnn_b_x2i, L2_gnn_W_h2h, L3_gnn_W_g1, L3_gnn_as_g1, L3_gnn_ad_g1, L3_gnn_b_g1, L3_gnn_W_g2, L3_gnn_as_g2, L3_gnn_ad_g2, L3_gnn_b_g2, L3_gnn_W_gf, L3_gnn_b_gf, L3_gnn_W_m1, L3_gnn_b_m1, L3_gnn_g_m1, L3_gnn_be_m1, L3_gnn_W_m2, L3_gnn_b_m2, L3_gnn_g_m2, L3_gnn_be_m2, L3_gnn_W_m3, L3_gnn_b_m3, L3_gnn_g_m3, L3_gnn_be_m3, L3_gnn_W_f, L3_gnn_b_f):
    import jax
    import jax.numpy as jnp

    def _L0_gnn_ref(x, edge_index, W, att_src, att_dst, bias):
        import jax, jax.numpy as jnp
        import numpy as np
        N_NODES = 3125
        N_EDGES = 50000
        IN_DIM = 256
        HEADS = 4
        F_HEAD = 64
        NEG_SLOPE = 0.2
        N = x.shape[0]
        H, Fh = att_src.shape
        loops = jnp.arange(N, dtype=edge_index.dtype)
        src = jnp.concatenate([edge_index[0], loops])
        dst = jnp.concatenate([edge_index[1], loops])
        h = jnp.einsum('nd,hdf->nhf', x, W)
        a_src = jnp.einsum('nhf,hf->nh', h, att_src)
        a_dst = jnp.einsum('nhf,hf->nh', h, att_dst)
        e = jax.nn.leaky_relu(a_src[src] + a_dst[dst], NEG_SLOPE)
        emax = jax.lax.stop_gradient(jax.ops.segment_max(e, dst, num_segments=N))
        ex = jnp.exp(e - emax[dst])
        denom = jax.ops.segment_sum(ex, dst, num_segments=N)
        alpha = ex / denom[dst]
        msg = h[src] * alpha[:, :, None]
        out = jax.ops.segment_sum(msg, dst, num_segments=N)
        return out.reshape(N, H * Fh) + bias

    def _L1_gnn_ref(x, rbf, Wf1, bf1, Wf2, bf2, Wu1, bu1, Wu2, bu2, gamma, beta, ei):
        import jax, jax.numpy as jnp
        import numpy as np
        N, E, HDIM, NG = (625, 20000, 256, 20)
        BN_EPS = 1e-05
        row, col = (ei[0], ei[1])
        filt = jax.nn.silu(rbf @ Wf1 + bf1) @ Wf2 + bf2
        msg = x[col] * filt
        agg = jax.ops.segment_sum(msg, row, num_segments=x.shape[0])
        h = jax.nn.silu(agg @ Wu1 + bu1) @ Wu2 + bu2
        mean = jnp.mean(h, axis=0)
        var = jnp.mean(jnp.square(h - mean), axis=0)
        bn = gamma * (h - mean) * jax.lax.rsqrt(var + BN_EPS) + beta
        return x + bn

    def _L2_gnn_ref(feat, src, dst, iw, ow, gamma, beta, W_in, b_in, W_out, b_out, W_x2i, b_x2i, W_h2h):
        import jax, jax.numpy as jnp
        import numpy as np
        N_NODES = 6250
        N_EDGES = 50000
        DIM = 256
        EPS = 1e-05
        N = feat.shape[0]
        num_steps = 1
        mean = jnp.mean(feat, axis=0)
        var = jnp.var(feat, axis=0)
        h = (feat - mean) * jax.lax.rsqrt(var + EPS) * gamma + beta
        for _ in range(num_steps):
            feat_in = h @ W_in + b_in
            feat_out = h @ W_out + b_out
            a_in = jax.ops.segment_sum(feat_in[src] * iw[:, None], dst, num_segments=N)
            a_out = jax.ops.segment_sum(feat_out[dst] * ow[:, None], src, num_segments=N)
            a = jnp.concatenate((a_in, a_out), axis=1)
            xi = a @ W_x2i + b_x2i
            hh = h @ W_h2h
            i_i, i_n = jnp.split(xi, 2, axis=1)
            h_i, h_n = jnp.split(hh, 2, axis=1)
            input_gate = jax.nn.sigmoid(i_i + h_i)
            new_gate = jnp.tanh(i_n + h_n)
            h = new_gate + input_gate * (h - new_gate)
        return h

    def _L3_gnn_ref(x, edge_index, W_g1, as_g1, ad_g1, b_g1, W_g2, as_g2, ad_g2, b_g2, W_gf, b_gf, W_m1, b_m1, g_m1, be_m1, W_m2, b_m2, g_m2, be_m2, W_m3, b_m3, g_m3, be_m3, W_f, b_f):
        import jax, jax.numpy as jnp
        import numpy as np
        N_NODES = 3125
        N_EDGES = 100000
        IN_CH = 256
        LAT = 32
        HID = 64
        OUT_CH = 256
        GAT_H = 32

        def _bn_relu(h, g, b):
            m = jnp.mean(h, axis=0)
            v = jnp.var(h, axis=0)
            return jax.nn.relu((h - m) * jax.lax.rsqrt(v + 1e-05) * g + b)

        def _gat(h_in, src, dst, W, a_s, a_d, b):
            N = h_in.shape[0]
            h = h_in @ W
            e = jax.nn.leaky_relu((h @ a_s)[src] + (h @ a_d)[dst], 0.2)
            m = jax.ops.segment_max(e, dst, num_segments=N)
            ex = jnp.exp(e - m[dst])
            den = jax.ops.segment_sum(ex, dst, num_segments=N)
            alpha = ex / den[dst]
            out = jax.ops.segment_sum(alpha[:, None] * h[src], dst, num_segments=N)
            return out + b
        N = x.shape[0]
        loops = jnp.arange(N)
        src = jnp.concatenate([edge_index[0], loops])
        dst = jnp.concatenate([edge_index[1], loops])
        r = _bn_relu(x @ W_m1 + b_m1, g_m1, be_m1)
        r = _bn_relu(r @ W_m2 + b_m2, g_m2, be_m2)
        r = _bn_relu(r @ W_m3 + b_m3, g_m3, be_m3)
        h = jax.nn.relu(_gat(x, src, dst, W_g1, as_g1, ad_g1, b_g1))
        h = jax.nn.relu(_gat(h, src, dst, W_g2, as_g2, ad_g2, b_g2))
        h = h @ W_gf + b_gf
        out = 0.5 * r + 0.5 * h
        return jax.nn.relu(out @ W_f + b_f)
    edge_index = jnp.stack([src, dst])
    h = jnp.maximum(_layernorm(x, axis=-1), 0.0)
    x = x + _L0_gnn_ref(h, edge_index, L0_gnn_W, L0_gnn_att_src, L0_gnn_att_dst, L0_gnn_bias)
    h = jnp.maximum(_layernorm(x, axis=-1), 0.0)
    x = x + _L1_gnn_ref(h, edge_attr_20, L1_gnn_Wf1, L1_gnn_bf1, L1_gnn_Wf2, L1_gnn_bf2, L1_gnn_Wu1, L1_gnn_bu1, L1_gnn_Wu2, L1_gnn_bu2, L1_gnn_gamma, L1_gnn_beta, edge_index)
    h = jnp.maximum(_layernorm(x, axis=-1), 0.0)
    x = x + _L2_gnn_ref(h, src, dst, edge_weight, edge_weight_n2, L2_gnn_gamma, L2_gnn_beta, L2_gnn_W_in, L2_gnn_b_in, L2_gnn_W_out, L2_gnn_b_out, L2_gnn_W_x2i, L2_gnn_b_x2i, L2_gnn_W_h2h)
    h = jnp.maximum(_layernorm(x, axis=-1), 0.0)
    x = x + _L3_gnn_ref(h, edge_index, L3_gnn_W_g1, L3_gnn_as_g1, L3_gnn_ad_g1, L3_gnn_b_g1, L3_gnn_W_g2, L3_gnn_as_g2, L3_gnn_ad_g2, L3_gnn_b_g2, L3_gnn_W_gf, L3_gnn_b_gf, L3_gnn_W_m1, L3_gnn_b_m1, L3_gnn_g_m1, L3_gnn_be_m1, L3_gnn_W_m2, L3_gnn_b_m2, L3_gnn_g_m2, L3_gnn_be_m2, L3_gnn_W_m3, L3_gnn_b_m3, L3_gnn_g_m3, L3_gnn_be_m3, L3_gnn_W_f, L3_gnn_b_f)
    return x

_drawn_inputs = setup_inputs


def setup_inputs(seed=0):
    import zlib

    import numpy as np

    out = dict(_drawn_inputs(seed))
    spreads = {'L0_gnn_bias': (0.0, 0.1),
     'L1_gnn_bf1': (0.0, 0.1),
     'L1_gnn_bf2': (0.0, 0.1),
     'L1_gnn_bu1': (0.0, 0.728),
     'L1_gnn_bu2': (0.0, 2.0),
     'L1_gnn_gamma': (1.0, 0.2),
     'L1_gnn_beta': (0.0, 0.1),
     'L2_gnn_gamma': (1.0, 0.2),
     'L2_gnn_beta': (0.0, 0.1),
     'L3_gnn_b_g1': (0.0, 0.8),
     'L3_gnn_b_g2': (0.0, 0.8),
     'L3_gnn_b_gf': (0.0, 2.0),
     'L3_gnn_b_m1': (0.0, 2.0),
     'L3_gnn_g_m1': (1.0, 0.6),
     'L3_gnn_be_m1': (0.0, 2.0),
     'L3_gnn_b_m2': (0.0, 2.0),
     'L3_gnn_g_m2': (1.0, 0.6),
     'L3_gnn_be_m2': (0.0, 2.0),
     'L3_gnn_b_m3': (0.0, 2.0),
     'L3_gnn_g_m3': (1.0, 0.6),
     'L3_gnn_be_m3': (0.0, 2.0),
     'L3_gnn_b_f': (0.0, 0.278)}
    factors = {'L0_gnn_att_dst': 6.419,
     'L2_gnn_b_x2i': 8.0,
     'L3_gnn_W_g1': 8.0,
     'L3_gnn_as_g1': 8.0,
     'L3_gnn_ad_g1': 8.0,
     'L3_gnn_W_g2': 8.0,
     'L3_gnn_as_g2': 8.0,
     'L3_gnn_ad_g2': 8.0,
     'L3_gnn_W_gf': 8.0,
     'L3_gnn_W_m3': 2.672}
    for name, (base, spread) in spreads.items():
        noise = np.random.default_rng([zlib.crc32(name.encode()), seed]).standard_normal(out[name].shape)
        drawn = base * np.exp(spread * noise) if base else spread * noise
        out[name] = jnp.asarray(drawn.astype(out[name].dtype))
    for name, factor in factors.items():
        out[name] = (out[name] * factor).astype(out[name].dtype)
    return out
```

```python
from contextlib import ExitStack

import concourse.bass as bass
from concourse import mybir

F32 = mybir.dt.float32
BF16 = mybir.dt.bfloat16
I32 = mybir.dt.int32
ALU = mybir.AluOpType
ACT = mybir.ActivationFunctionType
AX = mybir.AxisListType.X

N = 3125
E = 103125
D = 256
P = 125
NT = N // P
EC = E // P
LANES = 128
TG = 4
SLOTS = 4
T = -(-((E + NT * (LANES - 1)) // LANES) // (TG * SLOTS)) * TG * SLOTS
NG = T // TG
NI = NG // SLOTS
RB = 20
HEADS, FH = 4, 64
G3 = 32
HID, LAT = 64, 32
NSL = 5
NNI = NT // NSL
SC = 25
SSL = 3
NSS = EC // SC
EPS = 1e-5
BIG = 1e30
SLOPE = 0.2

D_IDX, D_LO, D_W, D_REC = 0, 1, 2, 4
S_ONE, S_IDX, S_LO, S_W, S_REC = RB, RB + 1, RB + 2, RB + 3, RB + 4

MAX, SUM, FILT, WSUM = "max", "sum", "filter", "weighted sum"


def skewed(eng, turns, slots, stages):
    deepest = max(lag for _, lag in stages)
    assert deepest < slots
    peeled = min(turns, 2 if deepest else 1)
    for t in range(peeled):
        for s in range(slots):
            for stage, lag in stages:
                if t or s >= lag:
                    stage(t if s >= lag else t - 1, (s - lag) % slots)
    if turns > peeled:
        with eng.Fori(peeled, turns) as i:
            for s in range(slots):
                for stage, lag in stages:
                    stage(i if s >= lag else i - 1, (s - lag) % slots)
    for s in range(deepest):
        for stage, lag in stages:
            if s < lag:
                stage(turns - 1, s - lag + slots)


def first(it):
    return isinstance(it, int) and it == 0


def gnn_kernel(nc, x, src, dst, edge_attr_20, edge_weight, edge_weight_n2, w, out):
    ctx = ExitStack()
    with ctx:
        def sb(name, shape, dt=F32):
            return ctx.enter_context(nc.sbuf_tensor(name, shape, dt))

        def sem(name):
            return ctx.enter_context(nc.semaphore(name))

        def dram(name, shape):
            return nc.dram_tensor(name, shape, F32, kind="Internal").ap()

        slots_d = dram("slots_by_dst", (LANES * T, D_REC))
        slots_s = dram("slots_by_src", (LANES * T, S_REC))
        t_as = dram("table_src_score", (N, HEADS))
        t_h = dram("table_heads", (N, D))
        t_x1 = dram("table_x1", (N, D))
        t_fo = dram("table_feat_out", (N, D))
        t_fi = dram("table_feat_in", (N, D))
        t_g1 = dram("table_gat1", (N, G3 + 1))
        t_g2 = dram("table_gat2", (N, G3 + 1))
        d_aout = dram("spilled_a_out", (N, D))
        d_x = dram("spilled_x", (N, D))
        d_lat = dram("spilled_lat", (LAT, N))
        vd = slots_d.rearrange("(p t) c -> p t c", t=T)
        vs = slots_s.rearrange("(p t) c -> p t c", t=T)

        TABW = D + 2 * HEADS
        AR = T * (G3 + 1)
        arena = sb("arena", [LANES, AR])
        o_r0, o_x = 0, NT * TABW
        o_r1 = o_x + NT * D
        o_hg = o_r1 + NT * TABW
        o_msg = o_hg + SLOTS * TG * D
        assert o_msg + 2 * TG * (D + HEADS) <= AR

        def view(off, rows, n):
            return arena[0:rows, off:off + n]

        acc0 = view(o_r0, P, NT * (D + HEADS)).rearrange("p (i f) -> p i f", f=D + HEADS)
        xs = view(o_x, P, NT * D).rearrange("p (i f) -> p i f", f=D)
        tab = view(o_r1, P, NT * TABW).rearrange("p (i f) -> p i f", f=TABW)
        as_e = view(o_r1, LANES, T * HEADS).rearrange("p (t h) -> p t h", h=HEADS)
        r0 = view(o_r0, P, NT * D).rearrange("p (i f) -> p i f", f=D)
        r1 = view(o_r1, P, NT * D).rearrange("p (i f) -> p i f", f=D)
        r0T = view(o_r0, LANES, 2 * N).rearrange("p (c n) -> p c n", c=2)
        r1T = view(o_r1, LANES, 2 * N).rearrange("p (c n) -> p c n", c=2)
        hg = view(o_hg, LANES, SLOTS * TG * D).rearrange("p (s j f) -> p s j f", s=SLOTS, j=TG)
        msg = view(o_msg, LANES, 2 * TG * (D + HEADS)).rearrange("p (s j f) -> p s j f", s=2, j=TG)
        keep3 = arena[:, :].rearrange("p (t f) -> p t f", f=G3 + 1)
        fio = view(o_hg, P, NSL * 2 * D).rearrange("p (s f) -> p s f", s=NSL)
        w_x2i = view(o_hg, LANES, 4 * 2 * D).rearrange("p (k m) -> p k m", k=4)
        w_h2h = view(o_hg + 8 * D, LANES, 2 * 2 * D).rearrange("p (k m) -> p k m", k=2)
        ai = view(o_msg, P, NSL * D).rearrange("p (s f) -> p s f", s=NSL)
        m1T, m2T, latT = view(o_r1, HID, N), view(o_r0, HID, N), view(o_r0 + N, LAT, N)

        def col(n, k=1):
            return view(n * EC, P, k * EC)

        aux_s = col(0, 4).rearrange("p (e c) -> p e c", c=4)
        aux_d = col(4, 4).rearrange("p (e c) -> p e c", c=4)
        hi = {"s": col(8), "d": col(9)}
        lo, mask, scan, rank, n_s, n_d, ew, ew2, adj = (col(10 + n) for n in range(9))
        pos = {"d": col(9), "s": col(8)}
        spare = [19 * EC]
        assert spare[0] <= o_hg

        o_up = [o_hg]

        def upper(rows, n):
            o_up[0] += n
            assert o_up[0] <= AR
            return view(o_up[0] - n, rows, n)

        FILL = T // 16
        fill_s = upper(LANES, FILL * S_REC).rearrange("p (t c) -> p t c", c=S_REC)
        fill_d = upper(LANES, FILL * D_REC).rearrange("p (t c) -> p t c", c=D_REC)
        tile_i, tile_f, bsum = upper(1, T).bitcast(I32), upper(1, T), upper(1, T)
        ints, ints2 = upper(P, EC).bitcast(I32), upper(P, EC).bitcast(I32)
        att = upper(LANES, 2 * D).rearrange("p (n f) -> p n f", n=2)
        att3 = upper(LANES, 4 * G3).rearrange("p (n f) -> p n f", n=4)
        wtmp = upper(LANES, D)

        iota_i = sb("iota_i", [LANES, LANES], I32)
        iota = sb("iota", [LANES, LANES])
        idn = sb("idn", [LANES, LANES])
        idn4 = sb("idn4", [LANES, HEADS, LANES], BF16)
        ones = sb("ones", [LANES, LANES])
        utri = sb("utri", [P, P])
        bkt = {"d": sb("bucket_d", [1, T], I32), "s": sb("bucket_s", [1, T], I32)}
        cnt, base = sb("cnt", [P, NT]), sb("base", [P, NT])
        tot_i, til_i = sb("tot_i", [LANES, NT], I32), sb("til_i", [LANES, NT], I32)
        til, ends, start = (sb(n, [LANES, NT]) for n in ("til", "ends", "start"))
        posi = sb("posi", [P, SSL, SC], I32)

        pay = sb("pay", [LANES, SLOTS, TG * S_REC])
        pay_d = pay[:, :, 0:TG * D_REC].rearrange("p s (j c) -> p s j c", c=D_REC)
        pay_s = pay[:, :, :].rearrange("p s (j c) -> p s j c", c=S_REC)
        idxi = sb("idxi", [LANES, SLOTS, TG], I32)
        oh = sb("onehot", [LANES, SLOTS, TG, P])
        ohb = sb("onehot_mask", [LANES, SLOTS, TG, P], BF16)
        ot = sb("onehot_T", [LANES, 2, TG, LANES])
        rT = ot[0:RB + 1, :, :, :].rearrange("p s j e -> p s (j e)")
        wide = sb("wide", [LANES, 4 * TG * LANES])
        hidT = wide[:, :].rearrange("p (s c e) -> p s c e", s=2, c=2)
        stage = wide[0:P, 0:SSL * SC * S_REC].rearrange("p (s e) -> p s e", s=SSL)
        gu = wide[:, 0:NSL * 2 * P].rearrange("p (s c n) -> p s c n", s=NSL, c=2)
        aT = wide[:, 0:4 * P].rearrange("p (c n) -> p c n", c=4)
        gT = wide[:, 4 * P:8 * P].rearrange("p (c n) -> p c n", c=4)
        tm = sb("tm", [P, SLOTS, TG, HEADS])
        mx = sb("mx", [P, NT, HEADS])
        adm = sb("adm", [P, NT, 2 * HEADS])
        arg = sb("arg", [LANES, 2, TG, HEADS])
        hg3 = sb("hg3", [LANES, SLOTS, TG, G3 + 1])
        msg3 = sb("msg3", [LANES, 2, TG, G3 + 1])
        acc3 = sb("acc3", [P, NT, G3 + 1])
        tb3 = sb("tb3", [P, NT, G3 + 2])
        den = sb("den", [P, NT, HEADS])
        own = sb("own", [P, NT, HEADS])
        hs = sb("hs", [P, NSL, D])
        tT = sb("tT", [LANES, NSL, 2, P])
        onT = sb("onT", [LAT + 1, NSL, P])
        st = sb("st", [LANES, 2, NT, 6])
        lst = sb("lst", [P, NT, 6])
        lmean, lvar, lrstd, lnb = (sb(n, [P, NT]) for n in ("lmean", "lvar", "lrstd", "lnb"))
        mv, bsc, bsh = sb("mv", [LANES, 2, 2]), sb("bsc", [LANES, 2]), sb("bsh", [LANES, 2])
        ones3 = sb("ones3", [3, LANES], BF16)
        bparts, bf2p = sb("bparts", [1, 3, D], BF16), sb("bf2p", [3, D], BF16)
        brow = sb("brow", [1, 2, D])

        wx0 = sb("wx0", [LANES, 2, TABW])
        wf1 = sb("wf1", [RB + 1, D])
        wf2, wu1, wu2 = (sb(n, [LANES, 2, D]) for n in ("wf2", "wu1", "wu2"))
        wio = sb("wio", [LANES, 2, 2 * D])
        wm1, wg1 = sb("wm1", [LANES, 2, HID]), sb("wg1", [LANES, 2, G3 + 2])
        wm2, wm3 = sb("wm2", [HID, LANES]), sb("wm3", [HID, LANES])
        wg2, wgf, wf = sb("wg2", [G3, G3 + 2]), sb("wgf", [G3, LANES]), sb("wf", [LAT + 1, D])
        bias0, bias_io, bg = sb("bias0", [P, D]), sb("bias_io", [P, 2 * D]), sb("bg", [P, 2, G3])
        cols = sb("cols", [LANES, 16])
        cols3 = sb("cols3", [HID, 10])

        ps = [ctx.enter_context(nc.psum_tensor(f"ps{n}", [128, 512], F32)) for n in range(8)]

        def turned_at(sl, rows=LANES, banks=3):
            return ps[sl % banks][0:rows, 0:2 * P].rearrange("p (c n) -> p c n", c=2)

        def second_at(sl):
            return ps[2 + sl % 3]

        def third_at(sl):
            return ps[5 + sl % 3]

        PH = [
            dict(kind=MAX, order="d", heads=HEADS, width=HEADS, table=t_as, ring=hg3),
            dict(kind=SUM, order="d", heads=HEADS, width=D, table=t_h, ring=hg, acc=acc0),
            dict(kind=FILT, order="s", width=D, table=t_x1, ring=hg, acc=r0),
            dict(kind=WSUM, order="s", width=D, table=t_fo, ring=hg, acc=r1),
            dict(kind=WSUM, order="d", width=D, table=t_fi, ring=hg, acc=r1),
            dict(kind=MAX, order="d", heads=1, width=G3 + 1, table=t_g1, ring=hg3),
            dict(kind=SUM, order="d", heads=1, width=G3, table=None, acc=acc3),
            dict(kind=MAX, order="d", heads=1, width=G3 + 1, table=t_g2, ring=hg3),
            dict(kind=SUM, order="d", heads=1, width=G3, table=None, acc=acc3),
        ]
        ALL = (MAX, SUM, FILT, WSUM)
        RATES = {
            "idx_ready": dict.fromkeys(ALL, 1),
            "onehot": dict.fromkeys(ALL, 1),
            "scattered": dict.fromkeys(ALL, TG),
            "acc_done": dict.fromkeys(ALL, TG),
            "reduced": {MAX: TG},
            "kept": {MAX: 1},
            "turned": {SUM: 1, FILT: 1},
            "turn_copied": {SUM: 1, FILT: 1},
            "dst_terms": {SUM: 1},
            "score_step": {SUM: 4},
            "exp_ready": {SUM: 1},
            "msg_ready": {SUM: 1, FILT: 2},
            "hidden": {FILT: 1},
            "hidden_act": {FILT: 1},
            "filtered": {FILT: 2},
        }
        esem = {n: sem(n) for n in RATES}
        loaded = [sem(f"loaded{s}") for s in range(SLOTS)]
        gathered = [sem(f"gathered{s}") for s in range(SLOTS)]

        def before(k, name):
            return sum(NG * RATES[name].get(p["kind"], 0) for p in PH[:k]
                       if name != "idx_ready" or p["table"] is not None)

        def gathers_before(k):
            return 16 * TG * NI * sum(p["table"] is not None for p in PH[:k])

        def wait_for(eng, k, name, it, sl, c=0, back=0):
            if sl < back:
                if first(it):
                    return
                it, sl = it - 1, sl + SLOTS
            r = RATES[name][PH[k]["kind"]]
            eng.wait_ge(esem[name], before(k, name) + r * SLOTS * it + r * (sl - back) + (c or r))

        def wait_loaded(eng, k, it, sl):
            eng.wait_ge(loaded[sl], 16 * NI * k + 16 * (it + 1))

        def wait_gathered(eng, k, it, sl):
            eng.wait_ge(gathered[sl], gathers_before(k) + 16 * TG * (it + 1))

        def phase_begins(eng, k):
            if k:
                eng.wait_ge(esem["acc_done"], before(k, "acc_done"))
                eng.wait_ge(esem["kept"], before(k, "kept"))

        def sum_at(k, j):
            ph = PH[k]
            if ph["kind"] == FILT:
                return ps[j // 2][0:P, D * (j % 2):D * (j % 2 + 1)]
            return ps[j][0:P, 0:ph["width"] + (ph["heads"] if ph["kind"] == SUM else 0)]

        s = {n: sem(n) for n in """consts consts_v w_small in_edges in_x filled blank w_late ln_stats link sort_step sort_go
             cnt_ready prefix_ready stage_cp sorted_d sorted_s att_ready table_ready table_spare spill lat_in
             pool_go sp_go parts_in""".split()}
        st_ld = [sem(f"st_ld{n}") for n in range(SSL)]
        scat = [sem(f"scat{n}") for n in range(SSL)]
        SCAT1 = 16 * SC * (NSS // SSL)
        NODE = dict(a=(0, 1, 2, 3, 5), t=(0, 2, 3, 4, 5, 8, 9), c=(0, 2, 3, 4, 5, 8, 9), m=(0, 3, 5, 6, 7, 8, 9),
                    o=(0, 8, 9), p=(2,), b=(2, 5, 6, 7, 9), q=(2, 8, 9), y=(2, 4, 9), j=(2, 3, 5, 6, 7),
                    h=(2, 3), g=(2, 4, 5), e=(2,), v=(3,), f=(3, 9), i=(4,), x=(4,), d=(4,), z=(4,), w=(9,))
        NODE_RATE = {"d4": 3, "f9": 2}
        node = {letter: sem(f"node_{letter}") for letter in NODE}
        slot_sem = {}

        def nsem(name):
            if name[1:].isdigit():
                assert int(name[1:]) in NODE[name[0]], name
                return node[name[0]]
            if name not in slot_sem:
                slot_sem[name] = sem(name)
            return slot_sem[name]

        def nbase(name):
            return sum(NT * NODE_RATE.get(f"{name[0]}{k}", 1) for k in NODE[name[0]] if k < int(name[1:]))

        def nwait(eng, name, it, sl, back=0, c=0):
            if sl < back:
                if first(it):
                    return
                it, sl = it - 1, sl + NSL
            r = NODE_RATE.get(name, 1)
            eng.wait_ge(nsem(name), nbase(name) + r * NSL * it + r * (sl - back) + (c or r))

        def all_tiles(eng, name):
            eng.wait_ge(nsem(name), nbase(name) + NT * NODE_RATE.get(name, 1))

        NORMS = ("ln0", "ln1", "bn1", "ln2", "bn2", "ln3", "bn5", "bn6", "bn7")
        ONCE = {"variance": NORMS, "deviation": NORMS, "norm": NORMS, "relu": ("r5", "r6", "r7"),
                "maxima": ("adm0", "adm5", "adm7"),
                "own_weight": ("adm0", "adm5", "adm7"), "attended": ("fin8", "fin9"), "taken": ("h0", "x1")}
        once = {kind: sem(kind) for kind in ONCE}

        def wait_once(eng, kind, name):
            eng.wait_ge(once[kind], ONCE[kind].index(name) + 1)

        def tiles(eng, *stages):
            skewed(eng, NNI, NSL, stages)

        def rows_of(i):
            return bass.ds(P * i, P)

        def flat(ap):
            return ap.rearrange("p a f -> p (a f)")

        def tile_no(it, sl):
            return NSL * it + sl

        def by_node(ap):
            return ap.rearrange("(i p) f -> p i f", p=P)

        W_LOADS = []

        def wload(to, frm):
            W_LOADS.append((to, frm))

        for c in range(2):
            a, b = c * LANES, (c + 1) * LANES
            wload(wx0[:, c, 0:D].rearrange("p (h f) -> p h f", h=HEADS),
                  w["L0_gnn_W"][:, a:b, :].rearrange("h p f -> p h f"))
            for to, name in ((wf2, "L1_gnn_Wf2"), (wu1, "L1_gnn_Wu1"), (wu2, "L1_gnn_Wu2"),
                             (wm1, "L3_gnn_W_m1")):
                wload(to[:, c, :], w[name][a:b, :])
            wload(wio[:, c, 0:D], w["L2_gnn_W_in"][a:b, :])
            wload(wio[:, c, D:2 * D], w["L2_gnn_W_out"][a:b, :])
            wload(wg1[:, c, 0:G3], w["L3_gnn_W_g1"][a:b, :])
        wload(wf1[0:RB, :], w["L1_gnn_Wf1"])
        wload(wf1[RB:RB + 1, :], w["L1_gnn_bf1"].unsqueeze(0))
        wload(brow[:, 0, :], w["L1_gnn_bf2"].unsqueeze(0))
        wload(att[:, 0, :], w["L0_gnn_att_src"].rearrange("h f -> (h f)").partition_broadcast(LANES))
        wload(att[:, 1, :], w["L0_gnn_att_dst"].rearrange("h f -> (h f)").partition_broadcast(LANES))
        for n, name in enumerate(["as_g1", "ad_g1", "as_g2", "ad_g2"]):
            wload(att3[:, n, :], w[f"L3_gnn_{name}"].partition_broadcast(LANES))
        wload(bias0[:, :], w["L0_gnn_bias"].partition_broadcast(P))
        wload(bias_io[:, 0:D], w["L2_gnn_b_in"].partition_broadcast(P))
        wload(bias_io[:, D:2 * D], w["L2_gnn_b_out"].partition_broadcast(P))
        wload(bg[:, 0, :], w["L3_gnn_b_g1"].partition_broadcast(P))
        wload(bg[:, 1, :], w["L3_gnn_b_g2"].partition_broadcast(P))
        wload(wm2[:, 0:HID], w["L3_gnn_W_m2"])
        wload(wm3[:, 0:LAT], w["L3_gnn_W_m3"])
        wload(wg2[:, 0:G3], w["L3_gnn_W_g2"])
        wload(wgf[:, 0:LAT], w["L3_gnn_W_gf"])
        wload(wf[0:LAT, :], w["L3_gnn_W_f"])
        wload(wf[LAT:LAT + 1, :], w["L3_gnn_b_f"].unsqueeze(0))
        for n, name in enumerate(["L1_gnn_bu1", "L1_gnn_bu2", "L1_gnn_gamma", "L1_gnn_beta",
                                  "L2_gnn_gamma", "L2_gnn_beta"]):
            for c in range(2):
                wload(cols[:, 2 * n + c:2 * n + c + 1], w[name][c * LANES:(c + 1) * LANES].unsqueeze(1))
        for c in range(4):
            wload(cols[:, 12 + c:13 + c], w["L2_gnn_b_x2i"][c * LANES:(c + 1) * LANES].unsqueeze(1))
        for n, name in enumerate(["b_m1", "g_m1", "be_m1", "b_m2", "g_m2", "be_m2"]):
            wload(cols3[:, n:n + 1], w[f"L3_gnn_{name}"].unsqueeze(1))
        for n, name in enumerate(["b_m3", "g_m3", "be_m3", "b_gf"]):
            wload(cols3[0:LAT, 6 + n:7 + n], w[f"L3_gnn_{name}"].unsqueeze(1))

        block = ctx.enter_context(nc.Block())

        @block.sync
        def _(sp):
            for to, frm in ((ints, dst), (ints2, src), (ew, edge_weight), (ew2, edge_weight_n2)):
                sp.dma_start(to, frm.rearrange("(p e) -> p e", e=EC)).then_inc(s["in_edges"], 16)
            sp.wait_ge(s["filled"], 1)
            for n in range(T // FILL):
                sp.dma_start(vd[:, n * FILL:(n + 1) * FILL, :], fill_d).then_inc(s["blank"], 16)
                sp.dma_start(vs[:, n * FILL:(n + 1) * FILL, :], fill_s).then_inc(s["blank"], 16)
            for to, frm in W_LOADS:
                sp.dma_start(to, frm).then_inc(s["w_small"], 16)

            av = edge_attr_20.rearrange("(p e) c -> p e c", e=EC)

            def attr(it, sl):
                sp.wait_ge(scat[sl], SCAT1 + 16 * SC * it)
                sp.sem_inc(s["sp_go"], 1)
                sp.dma_start(stage[:, sl, :].rearrange("p (e c) -> p e c", c=S_REC)[:, :, 0:RB],
                             av[:, bass.ds(SSL * SC * it + SC * sl, SC), :]).then_inc(st_ld[sl], 16)
            skewed(sp, NSS // SSL, SSL, [(attr, 0)])

            for sl in range(SSL):
                sp.wait_ge(scat[sl], 2 * SCAT1)
            sp.dma_start(xs, by_node(x)).then_inc(s["in_x"], 16)

            def edge_loads(k):
                ph = PH[k]
                phase_begins(sp, k)

                def load(it, sl):
                    wait_for(sp, k, "onehot", it, sl, back=SLOTS)
                    sp.sem_inc(s["sp_go"], 1)
                    if ph["table"] is not None:
                        wait_for(sp, k, "idx_ready", it, sl, back=SLOTS)
                        sp.sem_inc(s["sp_go"], 1)
                    if ph["kind"] == FILT:
                        wait_for(sp, k, "turned", it, sl, back=SLOTS)
                        sp.sem_inc(s["sp_go"], 1)
                    to, frm = (pay_d, vd) if ph["order"] == "d" else (pay_s, vs)
                    sp.dma_start(to[:, sl, :, :], frm[:, bass.ds(TG * SLOTS * it + TG * sl, TG), :])\
                      .then_inc(loaded[sl], 16)
                skewed(sp, NI, SLOTS, [(load, 0)])

            all_tiles(sp, "o0")
            sp.dma_start(by_node(t_h), tab[:, :, 0:D]).then_inc(s["table_ready"], 16)
            sp.dma_start(by_node(t_as), tab[:, :, D:D + HEADS]).then_inc(s["table_ready"], 16)
            sp.wait_ge(s["att_ready"], 1)
            for n in range(3):
                sp.dma_start(bf2p[n:n + 1, :], bparts[:, n, :]).then_inc(s["parts_in"], 16)
            edge_loads(0)
            edge_loads(1)
            all_tiles(sp, "a1")
            sp.dma_start(by_node(t_x1), r1).then_inc(s["table_ready"], 16)
            edge_loads(2)

            def feat(it, sl):
                nwait(sp, "f3", it, sl)
                sp.sem_inc(s["sp_go"], 1)
                i = tile_no(it, sl)
                sp.dma_start(t_fi[rows_of(i), :], fio[:, sl, 0:D]).then_inc(nsem(f"k3_{sl}"), 16)
                sp.dma_start(t_fo[rows_of(i), :], fio[:, sl, D:2 * D]).then_inc(nsem(f"k3_{sl}"), 16)
            tiles(sp, (feat, 0))
            edge_loads(3)
            sp.wait_ge(esem["acc_done"], before(4, "acc_done"))
            sp.dma_start(by_node(d_aout), r1).then_inc(s["spill"], 16)
            edge_loads(4)
            sp.wait_ge(esem["acc_done"], before(5, "acc_done"))
            sp.dma_start(w_x2i, w["L2_gnn_W_x2i"].rearrange("(k p) m -> p k m", p=LANES))\
              .then_inc(s["w_late"], 16)
            sp.dma_start(w_h2h, w["L2_gnn_W_h2h"].rearrange("(k p) m -> p k m", p=LANES))\
              .then_inc(s["w_late"], 16)

            def a_out(it, sl):
                nwait(sp, "t4", it, sl, back=NSL)
                sp.sem_inc(s["sp_go"], 1)
                sp.dma_start(hs[:, sl, :], d_aout[rows_of(tile_no(it, sl)), :]).then_inc(nsem(f"ld4_{sl}"), 16)
            sp.wait_ge(s["spill"], 16)
            tiles(sp, (a_out, 0))
            all_tiles(sp, "y4")
            sp.dma_start(by_node(d_x), xs).then_inc(s["spill"], 16)
            all_tiles(sp, "g5")
            sp.dma_start(by_node(t_g1), tb3[:, :, 0:G3 + 1]).then_inc(s["table_ready"], 16)
            wait_once(sp, "relu", "r7")
            sp.dma_start(d_lat, latT).then_inc(s["spill"], 16)
            edge_loads(5)
            edge_loads(6)
            all_tiles(sp, "o8")
            sp.dma_start(by_node(t_g2), tb3[:, :, 0:G3 + 1]).then_inc(s["table_ready"], 16)
            edge_loads(7)
            edge_loads(8)

            def x_back(it, sl):
                if not first(it):
                    sp.wait_ge(nsem(f"st9_{sl}"), 16 * it)
                    sp.sem_inc(s["sp_go"], 1)
                sp.dma_start(r1[:, sl, :], d_x[rows_of(tile_no(it, sl)), :]).then_inc(nsem(f"ld9_{sl}"), 16)

            def store(it, sl):
                nwait(sp, "y9", it, sl)
                sp.sem_inc(s["sp_go"], 1)
                sp.dma_start(out[rows_of(tile_no(it, sl)), :], r1[:, sl, :]).then_inc(nsem(f"st9_{sl}"), 16)
            sp.wait_ge(esem["acc_done"], before(9, "acc_done"))
            sp.dma_start(latT, d_lat).then_inc(s["lat_in"], 16)
            tiles(sp, (x_back, 0), (store, 3))
            for sl in range(NSL):
                sp.wait_ge(nsem(f"st9_{sl}"), 16 * NNI)

        @block.gpsimd
        def _(pool):
            nc.gpsimd.memset(fill_s, 0.0)
            nc.gpsimd.memset(fill_d, 0.0).then_inc(s["pool_go"], 1)
            pool.wait_ge(s["pool_go"], 1)
            nc.gpsimd.memset(fill_s[:, :, S_LO], -1.0)
            nc.gpsimd.memset(fill_d[:, :, D_LO], -1.0).then_inc(s["filled"], 1)
            nc.gpsimd.iota(iota_i[:, :], pattern=[[1, LANES]], base=0, channel_multiplier=0)
            nc.gpsimd.iota(tile_i, pattern=[[1, T]], base=0, channel_multiplier=0)
            nc.gpsimd.memset(idn[:, :], 0.0)
            nc.gpsimd.memset(utri[:, :], 0.0)
            nc.gpsimd.memset(ones[:, :], 1.0).then_inc(s["consts"], 1)
            pool.wait_ge(s["consts"], 1)
            nc.gpsimd.affine_select(out=idn[:, :], in_=idn[:, :], compare_op=ALU.not_equal, fill=1.0,
                                    base=0, pattern=[[-1, LANES]], channel_multiplier=1).then_inc(s["consts"], 1)
            nc.gpsimd.affine_select(out=utri[:, :], in_=utri[:, :], compare_op=ALU.is_ge, fill=1.0,
                                    base=0, pattern=[[-1, P]], channel_multiplier=1).then_inc(s["consts"], 1)

            def scatter(order, rec, dest):
                n0 = 0 if order == "d" else NSS

                def step(it, sl):
                    pool.wait_ge(s["stage_cp"], n0 + SSL * it + sl + 1)
                    pool.sem_inc(s["pool_go"], 1)
                    if order == "s":
                        pool.wait_ge(st_ld[sl], 16 * (it + 1))
                        pool.sem_inc(s["pool_go"], 1)
                    for c in range(SC):
                        pool.indirect_dma_start(
                            dest, bass.IndirectOffsetOnAxis(ap=posi[:, sl, c:c + 1], axis=0),
                            stage[:, sl, c * rec:(c + 1) * rec], None).then_inc(scat[sl], 16)
                skewed(pool, NSS // SSL, SSL, [(step, 0)])

            pool.wait_ge(s["blank"], 2 * 16 * (T // FILL))
            scatter("d", D_REC, slots_d)
            scatter("s", S_REC, slots_s)

            def gathers(k):
                ph = PH[k]
                phase_begins(pool, k)

                def step(it, sl):
                    wait_for(pool, k, "idx_ready", it, sl)
                    pool.sem_inc(s["pool_go"], 1)
                    if not first(it):
                        if ph["kind"] == MAX:
                            wait_for(pool, k, "kept", it, sl, back=SLOTS)
                            pool.sem_inc(s["pool_go"], 1)
                        wait_for(pool, k, "scattered" if ph["kind"] in (MAX, WSUM) else "msg_ready",
                                 it, sl, back=SLOTS)
                        pool.sem_inc(s["pool_go"], 1)
                    for j in range(TG):
                        pool.indirect_dma_start(
                            ph["ring"][:, sl, j, 0:ph["width"]], None, ph["table"],
                            bass.IndirectOffsetOnAxis(ap=idxi[:, sl, j:j + 1], axis=0))\
                            .then_inc(gathered[sl], 16)
                skewed(pool, NI, SLOTS, [(step, 0)])

            pool.wait_ge(s["table_ready"], 32)
            gathers(0)
            gathers(1)
            pool.wait_ge(s["table_ready"], 48)
            gathers(2)
            for sl in range(NSL):
                pool.wait_ge(nsem(f"k3_{sl}"), 32 * NNI)
            gathers(3)
            gathers(4)
            pool.wait_ge(s["table_ready"], 64)
            gathers(5)
            pool.wait_ge(s["table_ready"], 80)
            gathers(7)

        @block.scalar
        def _(act):
            A = nc.scalar.activation

            def stage_copies(order):
                aux, rec, off = (aux_d, D_REC, 0) if order == "d" else (aux_s, S_REC, RB)
                done = 0 if order == "d" else SCAT1
                act.wait_ge(s["sorted_" + order], 1)

                def step(it, sl):
                    if done or not first(it):
                        act.wait_ge(scat[sl], done + 16 * SC * it)
                    span = bass.ds(SSL * SC * it + SC * sl, SC)
                    A(stage[:, sl, 0:SC * rec].rearrange("p (e c) -> p e c", c=rec)[:, :, off:off + 4],
                      aux[:, span, :], ACT.Copy)
                    A(posi[:, sl, :], pos[order][:, span], ACT.Copy).then_inc(s["stage_cp"], 1)
                skewed(act, NSS // SSL, SSL, [(step, 0)])

            stage_copies("d")
            stage_copies("s")

            def normalised(it, sl, to):
                i = tile_no(it, sl)
                return A(to, flat(xs[:, bass.ds(i, 1), :]), ACT.Relu,
                         bias=lnb[:, bass.ds(i, 1)], scale=lrstd[:, bass.ds(i, 1)])

            def to_ring(name, freed_by):
                def stage_(it, sl):
                    nwait(act, freed_by, it, sl, back=NSL)
                    normalised(it, sl, hs[:, sl, :]).then_inc(nsem(name), 1)
                return stage_

            def norm_ready(name, ap):
                wait_once(act, "variance", name)
                A(ap, ap, ACT.Sqrt).then_inc(once["deviation"], 1)
                wait_once(act, "norm", name)

            def own_weight(H, name):
                wait_once(act, "maxima", name)
                A(own[:, :, 0:H], own[:, :, 0:H], ACT.Exp).then_inc(once["own_weight"], 1)

            def table0(it, sl):
                nwait(act, "m0", it, sl)
                A(flat(tab[:, bass.ds(tile_no(it, sl), 1), :]), ps[3 + sl][0:P, 0:TABW], ACT.Copy)\
                    .then_inc(nsem("o0"), 1)
            norm_ready("ln0", lrstd[:, :])
            tiles(act, (to_ring("a0", "t0"), 0), (table0, 3))

            def edges(k):
                ph = PH[k]
                kind, H, width = ph["kind"], ph.get("heads"), ph["width"]
                phase_begins(act, k)

                def indices(it, sl):
                    wait_loaded(act, k, it, sl)
                    if not first(it):
                        act.wait_ge(gathered[sl], gathers_before(k) + 16 * TG * it)
                    A(idxi[:, sl, :], pay_d[:, sl, :, D_IDX] if ph["order"] == "d" else pay_s[:, sl, :, S_IDX],
                      ACT.Copy).then_inc(esem["idx_ready"], 1)

                def keep(it, sl):
                    wait_gathered(act, k, it, sl)
                    to = as_e if H == HEADS else keep3
                    A(to[:, bass.ds(TG * SLOTS * it + TG * sl, TG), :], hg3[:, sl, :, 0:width], ACT.Copy)\
                        .then_inc(esem["kept"], 1)

                def turn_copy(it, sl):
                    wait_for(act, k, "turned", it, sl)
                    if kind == SUM:
                        wait_for(act, k, "dst_terms", it, sl, back=2)
                        A(ot[0:P, sl % 2, :, :], ps[4 + sl % 2][0:P, :].rearrange("p (j e) -> p j e", j=TG),
                          ACT.Copy).then_inc(esem["turn_copied"], 1)
                    else:
                        wait_for(act, k, "hidden", it, sl, back=2)
                        A(rT[:, sl % 2, :], ps[4][0:RB + 1, :], ACT.Copy).then_inc(esem["turn_copied"], 1)

                def exps(it, sl):
                    wait_for(act, k, "score_step", it, sl)
                    wait_for(act, k, "scattered", it, sl, back=2)
                    A((msg if H == HEADS else msg3)[:, sl % 2, :, width:width + H], arg[:, sl % 2, :, 0:H],
                      ACT.Exp).then_inc(esem["exp_ready"], 1)

                def silu(it, sl):
                    wait_for(act, k, "hidden", it, sl)
                    wait_for(act, k, "filtered", it, sl, back=2)
                    A(hidT[:, sl % 2, 0, :], ps[5][:, :], ACT.Silu)
                    A(hidT[:, sl % 2, 1, :], ps[6][:, :], ACT.Silu).then_inc(esem["hidden_act"], 1)

                stages = [(indices, 0)] if ph["table"] is not None else []
                stages += {MAX: [(keep, 3)], SUM: [(turn_copy, 0), (exps, 1)],
                           FILT: [(turn_copy, 0), (silu, 1)], WSUM: []}[kind]
                skewed(act, NI, SLOTS, stages)

            act.wait_ge(s["table_ready"], 32)
            wait_once(act, "taken", "h0")
            edges(0)
            own_weight(HEADS, "adm0")
            edges(1)

            def h1(it, sl):
                normalised(it, sl, flat(r1[:, bass.ds(tile_no(it, sl), 1), :])).then_inc(nsem("a1"), 1)
            norm_ready("ln1", lrstd[:, :])
            tiles(act, (h1, 0))
            edges(2)

            def agg(it, sl):
                nwait(act, "t2", it, sl, back=NSL)
                A(hs[:, sl, :], flat(r0[:, bass.ds(tile_no(it, sl), 1), :]), ACT.Copy).then_inc(nsem("a2"), 1)

            def silu_u(it, sl):
                nwait(act, "p2", it, sl)
                nwait(act, "q2", it, sl, back=NSL)
                A(gu[:, sl, 0, :], second_at(sl)[:, 0:P], ACT.Silu, bias=cols[:, 0:1])
                A(gu[:, sl, 1, :], second_at(sl)[:, P:2 * P], ACT.Silu, bias=cols[:, 1:2]).then_inc(nsem("b2"), 1)

            def bias_u(it, sl):
                nwait(act, "q2", it, sl)
                for c in range(2):
                    last = A(r1T[:, c, rows_of(tile_no(it, sl))], third_at(sl)[:, c * P:(c + 1) * P], ACT.Identity,
                             bias=cols[:, 2 + c:3 + c])
                last.then_inc(nsem("y2"), 1)
            act.wait_ge(esem["acc_done"], before(3, "acc_done"))
            wait_once(act, "taken", "x1")
            act.wait_ge(s["table_ready"], 48)
            tiles(act, (agg, 0), (silu_u, 2), (bias_u, 3))

            def affine(name, source, freed_by):
                def stage_(it, sl):
                    for f in freed_by:
                        nwait(act, f, it, sl, back=NSL)
                    for c in range(2):
                        last = A(tT[:, sl, c, :], source[:, c, rows_of(tile_no(it, sl))], ACT.Identity,
                                 bias=bsh[:, c:c + 1], scale=bsc[:, c:c + 1])
                    last.then_inc(nsem(name), 1)
                return stage_
            norm_ready("bn1", bsc[:, :])
            tiles(act, (affine("h2", r1T, ["g2"]), 0))

            norm_ready("ln2", lrstd[:, :])
            tiles(act, (to_ring("a3", "t3"), 0))
            norm_ready("bn2", bsc[:, :])
            tiles(act, (affine("h3", r0T, ["m3", "v3"]), 0))
            edges(3)
            edges(4)

            def a_in(it, sl):
                nwait(act, "t4", it, sl, back=NSL)
                A(ai[:, sl, :], flat(r1[:, bass.ds(tile_no(it, sl), 1), :]), ACT.Copy).then_inc(nsem("i4"), 1)

            def a_turned(it, sl):
                nwait(act, "t4", it, sl)
                nwait(act, "x4", it, sl, back=1)
                A(aT.rearrange("p c n -> p (c n)"), ps[0][:, 0:4 * P], ACT.Copy).then_inc(nsem("c4"), 1)

            def gates(it, sl):
                nwait(act, "x4", it, sl)
                nwait(act, "d4", it, sl, back=1)
                for c in range(4):
                    last = A(gT[:, c, :], ps[3 + sl][:, c * P:(c + 1) * P], ACT.Sigmoid if c < 2 else ACT.Tanh,
                             bias=cols[:, 12 + c:13 + c])
                last.then_inc(nsem("g4"), 1)
            act.wait_ge(esem["acc_done"], before(5, "acc_done"))
            tiles(act, (a_in, 0), (a_turned, 0), (gates, 1))

            def bias_stage(name, got, to, frm, bias):
                def stage_(it, sl):
                    nwait(act, got, it, sl)
                    A(to[:, rows_of(tile_no(it, sl))], frm(sl), ACT.Identity, bias=bias).then_inc(nsem(name), 1)
                return stage_

            def norm_relu(n, to, rows):
                norm_ready(f"bn{n}", bsc[0:rows, 0:1])
                A(to, to, ACT.Relu, bias=bsh[0:rows, 0:1], scale=bsc[0:rows, 0:1]).then_inc(once["relu"], 1)

            norm_ready("ln3", lrstd[:, :])
            tiles(act, (to_ring("a5", "t5"), 0),
                  (bias_stage("b5", "m5", m1T, lambda sl: third_at(sl)[0:HID, 0:P], cols3[:, 0:1]), 2))
            norm_relu(5, m1T, HID)
            tiles(act, (bias_stage("b6", "m6", m2T, lambda sl: ps[sl][0:HID, 0:P], cols3[:, 3:4]), 0))
            norm_relu(6, m2T, HID)
            tiles(act, (bias_stage("b7", "m7", latT, lambda sl: ps[sl][0:LAT, 0:P], cols3[0:LAT, 6:7]), 0))
            norm_relu(7, latT, LAT)

            def relu_out(name, freed_by):
                def stage_(it, sl):
                    nwait(act, freed_by, it, sl, back=NSL)
                    A(hs[:, sl, 0:G3], flat(acc3[:, bass.ds(tile_no(it, sl), 1), 0:G3]), ACT.Relu)\
                        .then_inc(nsem(name), 1)
                return stage_
            act.wait_ge(s["spill"], 48)
            edges(5)
            own_weight(1, "adm5")
            edges(6)
            wait_once(act, "attended", "fin8")
            tiles(act, (relu_out("q8", "t8"), 0))
            edges(7)
            own_weight(1, "adm7")
            edges(8)

            def gf_bias(it, sl):
                nwait(act, "m9", it, sl)
                nwait(act, "f9", it, sl, back=NSL)
                A(tT[0:LAT, sl, 1, :], ps[3 + sl][0:LAT, 256:256 + P], ACT.Identity, bias=cols3[0:LAT, 9:10])\
                    .then_inc(nsem("b9"), 1)

            def out_relu(it, sl):
                nwait(act, "o9", it, sl)
                A(hs[:, sl, :], ps[3 + sl][0:P, 0:D], ACT.Relu).then_inc(nsem("w9"), 1)
            wait_once(act, "attended", "fin9")
            tiles(act, (relu_out("q9", "y9"), 0), (gf_bias, 2), (out_relu, 3))

        @block.tensor
        def _(pe):
            MM = nc.tensor.matmul

            pe.wait_ge(s["consts"], 3)
            for n in range(2):
                pe.wait_ge(s["cnt_ready"], n + 1)
                MM(ps[0][0:P, 0:NT], utri[:, :], cnt[:, :], start=True, stop=True)
                MM(ps[0][:, 64:64 + NT], ones[0:P, :], cnt[:, :], start=True, stop=True)\
                    .then_inc(s["prefix_ready"], 1)

            def turn(name, got, freed_by, rows=2 * LANES, banks=3):
                def stage_(it, sl):
                    nwait(pe, got, it, sl)
                    nwait(pe, freed_by, it, sl, back=banks - 1)
                    if rows == G3:
                        last = nc.tensor.transpose(turned_at(sl, G3, banks)[:, 0, :], hs[:, sl, 0:G3], idn[0:P, 0:P])
                    else:
                        for c in range(2):
                            last = nc.tensor.transpose(turned_at(sl, LANES, banks)[:, c, :], hs[:, sl, c * LANES:(c + 1) * LANES],
                                                       idn[0:P, 0:P])
                    last.then_inc(nsem(name), 1)
                return stage_

            def table(name, got, freed_by, wide_w, width):
                def stage_(it, sl):
                    nwait(pe, got, it, sl)
                    nwait(pe, freed_by, it, sl, back=NSL)
                    for c in range(2):
                        last = MM(ps[3 + sl][0:P, 0:width], tT[:, sl, c, :], wide_w[:, c, :],
                                  start=(c == 0), stop=(c == 1))
                    last.then_inc(nsem(name), 1)
                return stage_

            pe.wait_ge(s["w_small"], 16 * len(W_LOADS))
            pe.wait_ge(s["att_ready"], 1)
            tiles(pe, (turn("t0", "a0", "c0"), 0), (table("m0", "c0", "o0", wx0, TABW), 1))

            def bucket(k, it, sl, j):
                at = TG * SLOTS * it + TG * sl + j
                return pe.value_load(bkt[PH[k]["order"]][0:1, bass.ds(at, 1)] if not isinstance(at, int)
                                     else bkt[PH[k]["order"]][0:1, at:at + 1], min_val=0, max_val=NT - 1)

            def edges(k):
                ph = PH[k]
                kind, H, width = ph["kind"], ph.get("heads"), ph["width"]
                total = width + (H if kind == SUM else 0)
                phase_begins(pe, k)

                def maxima(it, sl):
                    wait_for(pe, k, "onehot", it, sl)
                    wait_gathered(pe, k, it, sl)
                    a0 = 0 if H == HEADS else G3
                    for j in range(TG):
                        wait_for(pe, k, "reduced", it, sl, c=j + 1, back=1)
                        MM(ps[j][0:P, 0:H * LANES], ohb[:, sl, j, :],
                           idn4[:, 0:H, :].rearrange("p h e -> p (h e)"), start=True, stop=False)
                        for h in range(H):
                            last = MM(ps[j][0:P, h * LANES:(h + 1) * LANES],
                                      hg3[:, sl, j, a0 + h:a0 + h + 1].to_broadcast([LANES, P]), idn[:, :],
                                      start=False, stop=(h == H - 1))
                        last.then_inc(esem["scattered"], 1)

                def turn_onehot(it, sl):
                    wait_for(pe, k, "onehot", it, sl)
                    wait_for(pe, k, "turn_copied", it, sl, back=2)
                    for j in range(TG):
                        last = nc.tensor.transpose(ps[4 + sl % 2][0:P, j * LANES:(j + 1) * LANES],
                                                   oh[:, sl, j, :], idn[:, :])
                    last.then_inc(esem["turned"], 1)

                def dst_terms(it, sl):
                    wait_for(pe, k, "turn_copied", it, sl)
                    wait_for(pe, k, "score_step", it, sl, back=2)
                    for j in range(TG):
                        b = bucket(k, it, sl, j)
                        last = MM(ps[6 + sl % 2][:, 2 * HEADS * j:2 * HEADS * j + 2 * H],
                                  ot[0:P, sl % 2, j, :], flat(adm[:, bass.ds(b, 1), 0:2 * H]),
                                  start=True, stop=True)
                    last.then_inc(esem["dst_terms"], 1)

                def sums(it, sl):
                    if kind == WSUM:
                        wait_for(pe, k, "onehot", it, sl)
                        wait_gathered(pe, k, it, sl)
                        rows = hg[:, sl, :, :]
                    else:
                        rows = (msg if total > G3 + 1 else msg3)[:, sl % 2, :, 0:total]
                    for j in range(TG):
                        if kind == SUM and j == 0:
                            wait_for(pe, k, "msg_ready", it, sl)
                        if kind == FILT and j % 2 == 0:
                            wait_for(pe, k, "msg_ready", it, sl, c=j // 2 + 1)
                        if kind != FILT or j % 2 == 0:
                            wait_for(pe, k, "acc_done", it, sl, c=j + 1 + (kind == FILT), back=1)
                        MM(sum_at(k, j), oh[:, sl, j, :], rows[:, j, :], start=True, stop=True)\
                            .then_inc(esem["scattered"], 1)

                def turn_attr(it, sl):
                    wait_loaded(pe, k, it, sl)
                    wait_for(pe, k, "turn_copied", it, sl, back=1)
                    for j in range(TG):
                        last = nc.tensor.transpose(ps[4][0:RB + 1, j * LANES:(j + 1) * LANES],
                                                   pay_s[:, sl, j, 0:RB + 1], idn[:, :])
                    last.then_inc(esem["turned"], 1)

                def hidden(it, sl):
                    wait_for(pe, k, "turn_copied", it, sl)
                    wait_for(pe, k, "hidden_act", it, sl, back=1)
                    for c in range(2):
                        last = MM(ps[5 + c][:, :], wf1[:, c * LANES:(c + 1) * LANES], rT[:, sl % 2, :],
                                  start=True, stop=True)
                    last.then_inc(esem["hidden"], 1)

                def filt(it, sl):
                    wait_for(pe, k, "hidden_act", it, sl)
                    for half in range(2):
                        wait_for(pe, k, "msg_ready", it, sl, c=half + 1, back=1)
                        for j in (2 * half, 2 * half + 1):
                            to = ps[2 + half][:, D * (j % 2):D * (j % 2 + 1)]
                            for c in range(2):
                                MM(to, hidT[:, sl % 2, c, j * LANES:(j + 1) * LANES], wf2[:, c, :],
                                   start=(c == 0), stop=False)
                            last = MM(to, ones3[:, :], bf2p[:, :], start=False, stop=True)
                        last.then_inc(esem["filtered"], 1)

                if kind == FILT:
                    pe.wait_ge(s["parts_in"], 48)
                skewed(pe, NI, SLOTS,
                       {MAX: [(maxima, 0)], WSUM: [(sums, 0)],
                        SUM: [(turn_onehot, 0), (dst_terms, 1), (sums, 2)],
                        FILT: [(turn_attr, 0), (hidden, 1), (filt, 2), (sums, 3)]}[kind])

            edges(0)
            wait_once(pe, "maxima", "adm0")
            edges(1)
            edges(2)

            def mlp(name, got, freed_by, weight, source, to):
                def stage_(it, sl):
                    nwait(pe, got, it, sl)
                    nwait(pe, freed_by, it, sl, back=2)
                    for m in range(2):
                        for c in range(2):
                            last = MM(to(sl)[:, m * P:(m + 1) * P], weight[:, c, m * LANES:(m + 1) * LANES],
                                      source[:, sl, c, :], start=(c == 0), stop=(c == 1))
                    last.then_inc(nsem(name), 1)
                return stage_

            def turn_back(name, got, freed_by, at):
                def stage_(it, sl):
                    nwait(pe, got, it, sl)
                    nwait(pe, freed_by[0], it, sl, back=freed_by[1])
                    for c in range(2):
                        last = nc.tensor.transpose(at(sl)[0:P, c * LANES:(c + 1) * LANES], tT[:, sl, c, :],
                                                   idn[:, :])
                    last.then_inc(nsem(name), 1)
                return stage_
            tiles(pe, (turn("t2", "a2", "c2", banks=2), 0), (mlp("p2", "c2", "b2", wu1, tT, second_at), 1),
                  (mlp("q2", "b2", "y2", wu2, gu, third_at), 2))
            tiles(pe, (turn_back("g2", "h2", ("e2", NSL), lambda sl: ps[3 + sl]), 0))

            tiles(pe, (turn("t3", "a3", "c3"), 0))
            tiles(pe, (table("m3", "h3", "f3", wio, 2 * D), 0))
            edges(3)
            edges(4)

            def turn4(it, sl):
                nwait(pe, "i4", it, sl)
                pe.wait_ge(nsem(f"ld4_{sl}"), 16 * (it + 1))
                nwait(pe, "c4", it, sl, back=1)
                for c in range(4):
                    last = nc.tensor.transpose(ps[0][:, c * P:(c + 1) * P],
                                               (ai if c < 2 else hs)[:, sl, (c % 2) * LANES:(c % 2 + 1) * LANES],
                                               idn[0:P, 0:P])
                last.then_inc(nsem("t4"), 1)

            def gates(it, sl):
                nwait(pe, "c4", it, sl)
                nwait(pe, "g4", it, sl, back=NSL)
                for m in range(4):
                    cut = slice(m * LANES, (m + 1) * LANES)
                    for c in range(4):
                        MM(ps[3 + sl][:, m * P:(m + 1) * P], w_x2i[:, c, cut], aT[:, c, :],
                           start=(c == 0), stop=False)
                    for c in range(2):
                        last = MM(ps[3 + sl][:, m * P:(m + 1) * P], w_h2h[:, c, cut],
                                  r0T[:, c, rows_of(tile_no(it, sl))], start=False, stop=(c == 1))
                last.then_inc(nsem("x4"), 1)
            pe.wait_ge(s["w_late"], 32)
            tiles(pe, (turn4, 0), (gates, 1), (turn_back("z4", "d4", ("y4", 1), lambda sl: ps[1]), 2))

            def first3(it, sl):
                nwait(pe, "c5", it, sl)
                nwait(pe, "b5", it, sl, back=2)
                nwait(pe, "g5", it, sl, back=2)
                for c in range(2):
                    MM(second_at(sl)[0:P, 0:G3 + 2], tT[:, sl, c, :], wg1[:, c, :], start=(c == 0), stop=(c == 1))
                for c in range(2):
                    last = MM(third_at(sl)[0:HID, 0:P], wm1[:, c, :], tT[:, sl, c, :],
                              start=(c == 0), stop=(c == 1))
                last.then_inc(nsem("m5"), 1)
            tiles(pe, (turn("t5", "a5", "c5", banks=2), 0), (first3, 1))

            def mlp3(name, freed_by, weight, source):
                def stage_(it, sl):
                    nwait(pe, freed_by, it, sl, back=NSL)
                    MM(ps[sl][:, 0:P], weight[:, :], source[:, rows_of(tile_no(it, sl))],
                       start=True, stop=True).then_inc(nsem(name), 1)
                return stage_
            wait_once(pe, "relu", "r5")
            tiles(pe, (mlp3("m6", "b6", wm2, m1T), 0))
            wait_once(pe, "relu", "r6")
            tiles(pe, (mlp3("m7", "b7", wm3, m2T), 0))
            all_tiles(pe, "j7")
            edges(5)
            wait_once(pe, "maxima", "adm5")
            edges(6)

            def table2(it, sl):
                nwait(pe, "c8", it, sl)
                nwait(pe, "o8", it, sl, back=NSL)
                MM(ps[3 + sl][0:P, 0:G3 + 2], tT[0:G3, sl, 0, :], wg2[:, :], start=True, stop=True)\
                    .then_inc(nsem("m8"), 1)
            tiles(pe, (turn("t8", "q8", "c8", G3), 0), (table2, 1))
            edges(7)
            wait_once(pe, "maxima", "adm7")
            edges(8)

            def latent(it, sl):
                nwait(pe, "c9", it, sl)
                nwait(pe, "w9", it, sl, back=NSL)
                MM(ps[3 + sl][:, 256:256 + P], wgf[:, :], tT[0:G3, sl, 0, :], start=True, stop=True)\
                    .then_inc(nsem("m9"), 1)

            def last3(it, sl):
                nwait(pe, "f9", it, sl)
                MM(ps[3 + sl][0:P, 0:D], onT[:, sl, :], wf[:, :], start=True, stop=True).then_inc(nsem("o9"), 1)
            tiles(pe, (turn("t9", "q9", "c9", G3), 0), (latent, 1), (last3, 2))

        @block.vector
        def _(dve):
            V = nc.vector
            links = [0]

            def link(ins):
                links[0] += 1
                ins.then_inc(s["link"], 1)
                dve.wait_ge(s["link"], links[0])

            V.memset(ones3[:, :], 1.0)
            V.memset(wm2[:, HID:], 0.0)
            V.memset(wm3[:, LAT:], 0.0)
            V.memset(wgf[:, LAT:], 0.0)
            V.memset(onT[LAT:LAT + 1, :, :], 1.0)
            dve.wait_ge(s["consts"], 3)
            V.tensor_copy(iota[:, :], iota_i[:, :])
            V.tensor_copy(tile_f, tile_i)
            link(V.tensor_copy(idn4[:, :, :], idn[:, :].unsqueeze(1).to_broadcast([LANES, HEADS, LANES])))

            dve.wait_ge(s["in_edges"], 64)
            V.tensor_copy(n_d, ints)
            link(V.tensor_copy(n_s, ints2))

            def split(n, high, low):
                link(V.tensor_scalar(ints, n, 1.0 / P, None, ALU.mult))
                link(V.tensor_copy(high, ints))
                for op, add in ((ALU.is_ge, ALU.add), (ALU.is_lt, ALU.subtract)):
                    link(V.scalar_tensor_tensor(low, high, -float(P), n, ALU.mult, ALU.add))
                    link(V.tensor_scalar(adj, low, float(P) if op == ALU.is_ge else 0.0, None, op))
                    link(V.tensor_tensor(high, high, adj, add))
                link(V.scalar_tensor_tensor(low, high, -float(P), n, ALU.mult, ALU.add))

            def at(order_aux, c):
                return order_aux[:, :, c]

            split(n_d, hi["d"], lo)
            V.tensor_copy(at(aux_d, D_IDX), n_s)
            V.tensor_copy(at(aux_d, D_LO), lo)
            V.tensor_copy(at(aux_d, D_W), ew)
            link(V.memset(at(aux_d, 3), 0.0))
            split(n_s, hi["s"], lo)
            V.memset(at(aux_s, 0), 1.0)
            V.tensor_copy(at(aux_s, S_IDX - RB), n_d)
            V.tensor_copy(at(aux_s, S_LO - RB), lo)
            link(V.tensor_copy(at(aux_s, S_W - RB), ew2))

            steps = [0]

            def chain(ins, per, i, c):
                ins.then_inc(s["sort_step"], 1)
                dve.wait_ge(s["sort_step"], steps[0] + per * i + c)

            def sort(order, n):
                h = hi[order]
                with dve.Fori(0, NT) as b:
                    chain(V.tensor_scalar(mask, h, iota[0:P, bass.ds(b, 1)], None, ALU.is_equal), 2, b, 1)
                    chain(V.tensor_reduce(cnt[:, bass.ds(b, 1)], mask, AX, ALU.add), 2, b, 2)
                steps[0] += 2 * NT
                dve.sem_inc(s["cnt_ready"], 1)
                dve.wait_ge(s["prefix_ready"], n)
                link(V.tensor_scalar(tot_i[:, :], ps[0][:, 64:64 + NT], float(LANES - 1), None, ALU.add))
                link(V.tensor_scalar(til_i[:, :], tot_i[:, :], 7, None, ALU.logical_shift_right))
                link(V.tensor_copy(til[:, :], til_i[:, :]))
                link(V.tensor_tensor_scan(ends[:, :], til[:, :], til[:, :], 0.0, ALU.add, ALU.bypass))
                link(V.tensor_tensor(start[:, :], ends[:, :], til[:, :], ALU.subtract))
                link(V.scalar_tensor_tensor(base[:, :], start[0:P, :], float(LANES), ps[0][0:P, 0:NT],
                                            ALU.mult, ALU.add))
                link(V.memset(bsum, 0.0))
                with dve.Fori(1, NT) as b:
                    chain(V.scalar_tensor_tensor(bsum, tile_f, start[0:1, bass.ds(b, 1)], bsum,
                                                 ALU.is_ge, ALU.add), 1, b, 0)
                steps[0] += NT - 1
                link(V.tensor_copy(bkt[order][:, :], bsum))
                with dve.Fori(0, NT) as b:
                    chain(V.tensor_scalar(mask, h, iota[0:P, bass.ds(b, 1)], None, ALU.is_equal), 3, b, 1)
                    chain(V.tensor_tensor_scan(scan, mask, mask, base[:, bass.ds(b, 1)], ALU.add, ALU.bypass),
                          3, b, 2)
                    dve.sem_inc(s["sort_go"], 1)
                    chain(V.copy_predicated(rank, mask.bitcast(I32), scan), 3, b, 3)
                steps[0] += 3 * NT
                link(V.tensor_scalar(ints, rank, -1.0, None, ALU.add))
                link(V.tensor_scalar(ints2, ints, LANES - 1, None, ALU.bitwise_and))
                link(V.tensor_copy(scan, ints2))
                link(V.tensor_scalar(ints2, ints, 7, None, ALU.logical_shift_right))
                link(V.tensor_copy(rank, ints2))
                V.scalar_tensor_tensor(pos[order], scan, float(T), rank, ALU.mult, ALU.add)\
                    .then_inc(s["sorted_" + order], 1)
                dve.wait_ge(s["sorted_" + order], 1)

            sort("d", 1)
            sort("s", 2)

            dve.wait_ge(s["w_small"], 16 * len(W_LOADS))
            for c in range(2):
                for n in range(2):
                    link(V.tensor_tensor(wtmp, wx0[:, c, 0:D], att[:, n, :], ALU.mult))
                    link(V.tensor_reduce(wx0[:, c, D + HEADS * n:D + HEADS * (n + 1)],
                                         wtmp.rearrange("p (h f) -> p h f", h=HEADS), AX, ALU.add))
                    link(V.tensor_tensor(wtmp[:, 0:G3], wg1[:, c, 0:G3], att3[:, n, :], ALU.mult))
                    link(V.tensor_reduce(wg1[:, c, G3 + n:G3 + n + 1], wtmp[:, 0:G3], AX, ALU.add))
            for n in range(2):
                link(V.tensor_tensor(wtmp[0:G3, 0:G3], wg2[:, 0:G3], att3[0:G3, 2 + n, :], ALU.mult))
                link(V.tensor_reduce(wg2[:, G3 + n:G3 + n + 1], wtmp[0:G3, 0:G3], AX, ALU.add))
            link(V.tensor_copy(bparts[:, 0, :], brow[:, 0, :]))
            link(V.tensor_tensor(brow[:, 1, :], brow[:, 0, :], bparts[:, 0, :], ALU.subtract))
            link(V.tensor_copy(bparts[:, 1, :], brow[:, 1, :]))
            link(V.tensor_tensor(brow[:, 0, :], brow[:, 1, :], bparts[:, 1, :], ALU.subtract))
            V.tensor_copy(bparts[:, 2, :], brow[:, 0, :]).then_inc(s["att_ready"], 1)

            def layernorm(n):
                with dve.Fori(0, NT) as i:
                    V.bn_stats(flat(lst[:, bass.ds(i, 1), :]), flat(xs[:, bass.ds(i, 1), :])).then_inc(s["ln_stats"], 1)
                dve.wait_ge(s["ln_stats"], NT * (n + 1))
                even, odd = lst[:, :, 0:3], lst[:, :, 3:6]
                link(V.tensor_tensor(lmean[:, :], even[:, :, 1], odd[:, :, 1], ALU.add))
                link(V.tensor_scalar(lmean[:, :], lmean[:, :], 0.5, None, ALU.mult))
                link(V.tensor_tensor(lrstd[:, :], even[:, :, 1], odd[:, :, 1], ALU.subtract))
                link(V.scalar_tensor_tensor(lrstd[:, :], lrstd[:, :], 0.25, lrstd[:, :], ALU.mult, ALU.mult))
                link(V.tensor_tensor(lvar[:, :], even[:, :, 2], odd[:, :, 2], ALU.add))
                link(V.scalar_tensor_tensor(lvar[:, :], lvar[:, :], 1.0 / D, lrstd[:, :], ALU.mult, ALU.add))
                V.tensor_scalar(lrstd[:, :], lvar[:, :], EPS, None, ALU.add).then_inc(once["variance"], 1)
                wait_once(dve, "deviation", f"ln{n}")
                link(V.reciprocal(lrstd[:, :], lrstd[:, :]))
                V.scalar_tensor_tensor(lnb[:, :], lmean[:, :], -1.0, lrstd[:, :], ALU.mult, ALU.mult)\
                    .then_inc(once["norm"], 1)

            def turn_copy(name, got, freed_by, rows=LANES, chunks=2, banks=3):
                def stage_(it, sl):
                    nwait(dve, got, it, sl)
                    nwait(dve, freed_by, it, sl, back=NSL)
                    V.tensor_copy(tT[0:rows, sl, 0:chunks, :], turned_at(sl, rows, banks)[:, 0:chunks, :])\
                        .then_inc(nsem(name), 1)
                return stage_

            dve.wait_ge(s["in_x"], 16)
            layernorm(0)
            tiles(dve, (turn_copy("c0", "t0", "m0"), 0))
            all_tiles(dve, "o0")
            V.tensor_copy(adm[:, :, 0:HEADS], tab[:, :, D + HEADS:TABW])
            V.tensor_copy(acc0[:, :, 0:D], tab[:, :, 0:D])
            V.tensor_copy(mx[:, :, :], tab[:, :, D:D + HEADS])
            V.tensor_copy(own[:, :, :], tab[:, :, D:D + HEADS]).then_inc(once["taken"], 1)
            wait_once(dve, "taken", "h0")

            def bucket(k, it, sl, j):
                at_ = TG * SLOTS * it + TG * sl + j
                return dve.value_load(bkt[PH[k]["order"]][0:1, bass.ds(at_, 1)], min_val=0, max_val=NT - 1)

            def edges(k):
                ph = PH[k]
                kind, H, width = ph["kind"], ph.get("heads"), ph["width"]
                dorder = ph["order"] == "d"
                payload, c_lo, c_w = (pay_d, D_LO, D_W) if dorder else (pay_s, S_LO, S_W)
                phase_begins(dve, k)

                def onehots(it, sl):
                    wait_loaded(dve, k, it, sl)
                    wait_for(dve, k, "scattered", it, sl, back=SLOTS)
                    for j in range(TG):
                        low = payload[:, sl, j, c_lo:c_lo + 1]
                        if kind == MAX:
                            last = V.tensor_scalar(ohb[:, sl, j, :], iota[:, 0:P], low, -BIG,
                                                   ALU.not_equal, ALU.mult)
                        elif kind == WSUM:
                            last = V.tensor_scalar(oh[:, sl, j, :], iota[:, 0:P], low,
                                                   payload[:, sl, j, c_w:c_w + 1], ALU.is_equal, ALU.mult)
                        else:
                            last = V.tensor_scalar(oh[:, sl, j, :], iota[:, 0:P], low, None, ALU.is_equal)
                    last.then_inc(esem["onehot"], 1)

                def maxima(it, sl):
                    for j in range(TG):
                        wait_for(dve, k, "scattered", it, sl, c=j + 1)
                        V.tensor_reduce(tm[:, sl, j, 0:H], ps[j][0:P, 0:H * LANES]
                                        .rearrange("p (h e) -> p h e", h=H), AX, ALU.max)\
                            .then_inc(esem["reduced"], 1)
                    for j in range(TG):
                        wait_for(dve, k, "reduced", it, sl, c=j + 1)
                        added_before(it, sl, j)
                        m = flat(mx[:, bass.ds(bucket(k, it, sl, j), 1), 0:H])
                        V.tensor_tensor(m, m, tm[:, sl, j, 0:H], ALU.max).then_inc(esem["acc_done"], 1)

                def added_before(it, sl, j):
                    if not (first(it) and sl == 0 and j == 0):
                        if j:
                            wait_for(dve, k, "acc_done", it, sl, c=j)
                        else:
                            wait_for(dve, k, "acc_done", it, sl, back=1)

                def scores(it, sl):
                    wait_for(dve, k, "dst_terms", it, sl)
                    if H == HEADS:
                        source = as_e[:, bass.ds(TG * SLOTS * it + TG * sl, TG), :]
                    else:
                        source = keep3[:, bass.ds(TG * SLOTS * it + TG * sl, TG), G3:G3 + 1]
                    terms = ps[6 + sl % 2][:, 0:2 * HEADS * TG].rearrange("p (j c) -> p j c", j=TG)
                    a = arg[:, sl % 2, :, 0:H]
                    wait_for(dve, k, "exp_ready", it, sl, back=2)
                    V.tensor_tensor(a, source, terms[:, :, 0:H], ALU.add).then_inc(esem["score_step"], 1)
                    wait_for(dve, k, "score_step", it, sl, c=1)
                    V.scalar_tensor_tensor(a, a, SLOPE, a, ALU.mult, ALU.max).then_inc(esem["score_step"], 1)
                    wait_for(dve, k, "score_step", it, sl, c=2)
                    V.tensor_tensor(a, a, terms[:, :, H:2 * H], ALU.min).then_inc(esem["score_step"], 1)
                    wait_for(dve, k, "score_step", it, sl, c=3)
                    V.tensor_tensor(a, a, terms[:, :, H:2 * H], ALU.subtract).then_inc(esem["score_step"], 1)

                def messages(it, sl):
                    if kind == SUM:
                        wait_for(dve, k, "exp_ready", it, sl)
                        wait_for(dve, k, "scattered", it, sl, back=2)
                        if H == HEADS:
                            wait_gathered(dve, k, it, sl)
                            for j in range(TG):
                                last = V.tensor_tensor(
                                    msg[:, sl % 2, j, 0:D].rearrange("p (h f) -> p h f", h=H),
                                    hg[:, sl, j, :].rearrange("p (h f) -> p h f", h=H),
                                    msg[:, sl % 2, j, D:D + H].unsqueeze(2).to_broadcast([LANES, H, FH]), ALU.mult)
                        else:
                            last = V.tensor_tensor(
                                msg3[:, sl % 2, :, 0:G3], keep3[:, bass.ds(TG * SLOTS * it + TG * sl, TG), 0:G3],
                                msg3[:, sl % 2, :, G3:G3 + 1].to_broadcast([LANES, TG, G3]), ALU.mult)
                        last.then_inc(esem["msg_ready"], 1)
                        return
                    wait_gathered(dve, k, it, sl)
                    wait_for(dve, k, "scattered", it, sl, back=2)
                    for half in range(2):
                        wait_for(dve, k, "filtered", it, sl, c=half + 1)
                        V.tensor_tensor(msg[:, sl % 2, 2 * half:2 * half + 2, 0:D],
                                        ps[2 + half][:, :].rearrange("p (j f) -> p j f", j=2),
                                        hg[:, sl, 2 * half:2 * half + 2, :], ALU.mult)\
                            .then_inc(esem["msg_ready"], 1)

                def adds(it, sl):
                    for j in range(TG):
                        wait_for(dve, k, "scattered", it, sl, c=j // 2 * 2 + 2 if kind == FILT else j + 1)
                        added_before(it, sl, j)
                        a = flat(ph["acc"][:, bass.ds(bucket(k, it, sl, j), 1), :])
                        V.tensor_tensor(a, a, sum_at(k, j), ALU.add).then_inc(esem["acc_done"], 1)

                skewed(dve, NI, SLOTS,
                       {MAX: [(onehots, 0), (maxima, 1)], WSUM: [(onehots, 0), (adds, 2)],
                        SUM: [(onehots, 0), (scores, 1), (messages, 2), (adds, 3)],
                        FILT: [(onehots, 0), (messages, 2), (adds, 3)]}[kind])
                dve.wait_ge(esem["acc_done"], before(k + 1, "acc_done"))

            def bounds(H, name):
                m, a, o = adm[:, :, H:2 * H], adm[:, :, 0:H], own[:, :, 0:H]
                V.tensor_tensor(o, o, a, ALU.add)
                link(V.tensor_tensor(m, mx[:, :, 0:H], a, ALU.add))
                V.scalar_tensor_tensor(o, o, SLOPE, o, ALU.mult, ALU.max)
                link(V.scalar_tensor_tensor(m, m, SLOPE, m, ALU.mult, ALU.max))
                V.tensor_tensor(o, o, m, ALU.subtract).then_inc(once["maxima"], 1)
                wait_once(dve, "own_weight", name)

            edges(0)
            bounds(HEADS, "adm0")
            for h in range(HEADS):
                rows = acc0[:, :, h * FH:(h + 1) * FH]
                V.tensor_tensor(rows, rows, own[:, :, h:h + 1].to_broadcast([P, NT, FH]), ALU.mult)
            link(V.tensor_copy(acc0[:, :, D:D + HEADS], own[:, :, :]))
            edges(1)
            link(V.reciprocal(den[:, :, :], acc0[:, :, D:D + HEADS]))
            for h in range(HEADS):
                last = V.tensor_tensor(acc0[:, :, h * FH:(h + 1) * FH], acc0[:, :, h * FH:(h + 1) * FH],
                                       den[:, :, h:h + 1].to_broadcast([P, NT, FH]), ALU.mult)
            link(last)
            link(V.tensor_tensor(xs, xs, acc0[:, :, 0:D], ALU.add))
            link(V.tensor_tensor(xs, xs, bias0[:, :].unsqueeze(1).to_broadcast([P, NT, D]), ALU.add))

            layernorm(1)
            link(V.memset(r0, 0.0))
            all_tiles(dve, "a1")
            V.tensor_tensor(xs, xs, r1, ALU.add).then_inc(once["taken"], 1)
            edges(2)

            def node_stats(name, got, source, rows=LANES, chunks=2):
                def stage_(it, sl):
                    nwait(dve, got, it, sl)
                    i = tile_no(it, sl)
                    for c in range(chunks):
                        frm = source[:, c, rows_of(i)] if chunks == 2 else source[:, rows_of(i)]
                        last = V.bn_stats(flat(st[0:rows, c, bass.ds(i, 1), :]), frm)
                    last.then_inc(nsem(name), 1)
                return stage_

            def batchnorm(n, stats, gamma, beta, rows=LANES, chunks=2):
                all_tiles(dve, stats)
                for c in range(chunks):
                    last = V.bn_aggr(mv[0:rows, c, :], st[0:rows, c, :, :].rearrange("p i f -> p (i f)"))
                link(last)
                sc, sh = bsc[0:rows, 0:chunks], bsh[0:rows, 0:chunks]
                V.tensor_scalar(sc, mv[0:rows, 0:chunks, 1], EPS, None, ALU.add).then_inc(once["variance"], 1)
                wait_once(dve, "deviation", f"bn{n}")
                link(V.reciprocal(sc, sc))
                link(V.tensor_tensor(sc, sc, gamma, ALU.mult))
                link(V.tensor_tensor(sh, mv[0:rows, 0:chunks, 0], sc, ALU.mult))
                V.tensor_tensor(sh, beta, sh, ALU.subtract).then_inc(once["norm"], 1)

            tiles(dve, (turn_copy("c2", "t2", "p2", banks=2), 0), (node_stats("j2", "y2", r1T), 3))
            batchnorm(1, "j2", cols[:, 4:6], cols[:, 6:8])

            def x_add(name, got, at_):
                def stage_(it, sl):
                    nwait(dve, got, it, sl)
                    xt = flat(xs[:, bass.ds(tile_no(it, sl), 1), :])
                    V.tensor_tensor(xt, xt, at_(sl)[0:P, 0:D], ALU.add).then_inc(nsem(name), 1)
                return stage_
            tiles(dve, (x_add("e2", "g2", lambda sl: ps[3 + sl]), 0))

            all_tiles(dve, "e2")
            layernorm(2)

            def feat_T(it, sl):
                nwait(dve, "t3", it, sl)
                V.tensor_copy(r0T[:, :, rows_of(tile_no(it, sl))], turned_at(sl)).then_inc(nsem("c3"), 1)
            tiles(dve, (feat_T, 0), (node_stats("j3", "c3", r0T), 1))
            batchnorm(2, "j3", cols[:, 8:10], cols[:, 10:12])

            def normed_back(it, sl):
                nwait(dve, "h3", it, sl)
                V.tensor_copy(r0T[:, :, rows_of(tile_no(it, sl))], tT[:, sl, :, :]).then_inc(nsem("v3"), 1)

            def feat_bias(it, sl):
                nwait(dve, "m3", it, sl)
                if not first(it):
                    dve.wait_ge(nsem(f"k3_{sl}"), 32 * it)
                V.tensor_tensor(fio[:, sl, :], ps[3 + sl][0:P, :], bias_io[:, :], ALU.add).then_inc(nsem("f3"), 1)
            tiles(dve, (normed_back, 0), (feat_bias, 1))
            link(V.memset(r1, 0.0))
            edges(3)
            dve.wait_ge(s["spill"], 16)
            link(V.memset(r1, 0.0))
            edges(4)

            def blend(it, sl):
                nwait(dve, "g4", it, sl)
                nwait(dve, "z4", it, sl, back=NSL)
                ig, ng, o = gT[:, 0:2, :], gT[:, 2:4, :], tT[:, sl, :, :]
                h_ = r0T[:, :, rows_of(tile_no(it, sl))]
                for c, (a, b, op) in enumerate(((h_, ng, ALU.subtract), (o, ig, ALU.mult), (o, ng, ALU.add))):
                    if c:
                        nwait(dve, "d4", it, sl, c=c)
                    ins = V.tensor_tensor(o, a, b, op).then_inc(nsem("d4"), 1)
            tiles(dve, (blend, 0), (x_add("y4", "z4", lambda sl: ps[1]), 1))

            all_tiles(dve, "y4")
            layernorm(3)

            def table3(name, got, at_):
                def stage_(it, sl):
                    nwait(dve, got, it, sl)
                    V.tensor_copy(flat(tb3[:, bass.ds(tile_no(it, sl), 1), :]), at_(sl)[0:P, 0:G3 + 2])\
                        .then_inc(nsem(name), 1)
                return stage_
            tiles(dve, (turn_copy("c5", "t5", "m5", banks=2), 0), (table3("g5", "m5", second_at), 2),
                  (node_stats("j5", "b5", m1T, HID, 1), 3))
            batchnorm(5, "j5", cols3[:, 1:2], cols3[:, 2:3], HID, 1)
            tiles(dve, (node_stats("j6", "b6", m2T, HID, 1), 0))
            batchnorm(6, "j6", cols3[:, 4:5], cols3[:, 5:6], HID, 1)
            tiles(dve, (node_stats("j7", "b7", latT, LAT, 1), 0))
            batchnorm(7, "j7", cols3[0:LAT, 7:8], cols3[0:LAT, 8:9], LAT, 1)

            def attention(k, n):
                link(V.tensor_copy(adm[:, :, 0:1], tb3[:, :, G3 + 1:G3 + 2]))
                V.tensor_copy(mx[:, :, 0:1], tb3[:, :, G3:G3 + 1])
                link(V.tensor_copy(own[:, :, 0:1], tb3[:, :, G3:G3 + 1]))
                edges(k)
                bounds(1, f"adm{k}")
                V.tensor_copy(acc3[:, :, G3:G3 + 1], own[:, :, 0:1])
                link(V.tensor_tensor(acc3[:, :, 0:G3], tb3[:, :, 0:G3],
                                     own[:, :, 0:1].to_broadcast([P, NT, G3]), ALU.mult))
                edges(k + 1)
                link(V.reciprocal(den[:, :, 0:1], acc3[:, :, G3:G3 + 1]))
                rows = acc3[:, :, 0:G3]
                link(V.tensor_tensor(rows, rows, den[:, :, 0:1].to_broadcast([P, NT, G3]), ALU.mult))
                V.tensor_tensor(rows, rows, bg[:, n, :].unsqueeze(1).to_broadcast([P, NT, G3]), ALU.add)\
                    .then_inc(once["attended"], 1)

            attention(5, 0)
            tiles(dve, (turn_copy("c8", "t8", "m8", G3, 1), 0), (table3("o8", "m8", lambda sl: ps[3 + sl]), 1))
            all_tiles(dve, "o8")
            attention(7, 1)

            def blend3(it, sl):
                nwait(dve, "b9", it, sl)
                nwait(dve, "o9", it, sl, back=NSL)
                V.tensor_scalar(tT[0:LAT, sl, 1, :], tT[0:LAT, sl, 1, :], 0.5, None, ALU.mult)\
                    .then_inc(nsem("f9"), 1)
                nwait(dve, "f9", it, sl, c=1)
                V.scalar_tensor_tensor(onT[0:LAT, sl, :], latT[:, rows_of(tile_no(it, sl))], 0.5,
                                       tT[0:LAT, sl, 1, :], ALU.mult, ALU.add).then_inc(nsem("f9"), 1)

            def x_out(it, sl):
                nwait(dve, "w9", it, sl)
                dve.wait_ge(nsem(f"ld9_{sl}"), 16 * (it + 1))
                V.tensor_tensor(r1[:, sl, :], r1[:, sl, :], hs[:, sl, :], ALU.add).then_inc(nsem("y9"), 1)
            dve.wait_ge(s["lat_in"], 16)
            tiles(dve, (turn_copy("c9", "t9", "m9", G3, 1), 0), (blend3, 2), (x_out, 3))


_FIRST = ["x", "src", "dst", "edge_attr_20", "edge_weight", "edge_weight_n2"]
_WEIGHTS = (["L0_gnn_" + n for n in ("W", "att_src", "att_dst", "bias")]
            + ["L1_gnn_" + n for n in ("Wf1", "bf1", "Wf2", "bf2", "Wu1", "bu1", "Wu2", "bu2", "gamma", "beta")]
            + ["L2_gnn_" + n for n in ("gamma", "beta", "W_in", "b_in", "W_out", "b_out", "W_x2i", "b_x2i", "W_h2h")]
            + ["L3_gnn_" + n for n in (
                "W_g1", "as_g1", "ad_g1", "b_g1", "W_g2", "as_g2", "ad_g2", "b_g2", "W_gf", "b_gf", "W_m1", "b_m1",
                "g_m1", "be_m1", "W_m2", "b_m2", "g_m2", "be_m2", "W_m3", "b_m3", "g_m3", "be_m3", "W_f", "b_f")])


def kernel(**inputs):
    import numpy as _np
    import concourse.bacc as _bacc
    from concourse import mybir as _mybir
    from concourse.bass_utils import run_bass_kernel_spmd as _run

    nc = _bacc.Bacc("TRN2", target_bir_lowering=False, num_devices=1)
    arrays, aps = {}, {}
    for name in _FIRST + _WEIGHTS:
        a = _np.ascontiguousarray(inputs[name])
        arrays[f"in_{name}"] = a
        aps[name] = nc.dram_tensor(f"in_{name}", a.shape, _mybir.dt.from_np(a.dtype), kind="ExternalInput").ap()
    out = nc.dram_tensor("out_0", (N, D), F32, kind="ExternalOutput").ap()
    gnn_kernel(nc, *(aps[n] for n in _FIRST), {n: aps[n] for n in _WEIGHTS}, out)
    r = _run(nc, [arrays], core_ids=[0])
    return r.results[0]["out_0"]
```

```python
from contextlib import ExitStack

import concourse.bass as bass
from concourse import mybir

F32 = mybir.dt.float32
BF16 = mybir.dt.bfloat16
I32 = mybir.dt.int32
ALU = mybir.AluOpType
ACT = mybir.ActivationFunctionType
AX = mybir.AxisListType.X

N = 3125
E = 103125
D = 256
P = 125
NT = N // P
EC = E // P
LANES = 128
TG = 4
SLOTS = 4
GE = TG * LANES
NG = -(-((E + NT * (GE - 1)) // GE) // SLOTS) * SLOTS
T = NG * TG
NI = NG // SLOTS
RB = 20
HEADS, FH = 4, 64
G3 = 32
HID, LAT = 64, 32
NSL = 5
NNI = NT // NSL
SC = 25
SSL = 3
NSS = EC // SC
S_NODES = 5
EPS = 1e-5
BIG = 1e30
SLOPE = 0.2

D_IDX, D_LO, D_W, D_REC = 0, 1, 2, 4
S_ONE, S_IDX, S_LO, S_W, S_REC = RB, RB + 1, RB + 2, RB + 3, RB + 4

A_PART = (0, 0, 0, 1, 1, 2)
W_PART = (0, 1, 2, 0, 1, 0)
RK = len(A_PART) * (RB + 1)

MAX, MAX1, SUM, FILT, WSUM = "max", "max of one head", "sum", "filter", "weighted sum"


def skewed(eng, turns, slots, stages):
    deepest = max(lag for _, lag in stages)
    assert deepest < slots
    peeled = min(turns, 2 if deepest else 1)
    for t in range(peeled):
        for s in range(slots):
            for stage, lag in stages:
                if t or s >= lag:
                    stage(t if s >= lag else t - 1, (s - lag) % slots)
    if turns > peeled:
        with eng.Fori(peeled, turns) as i:
            for s in range(slots):
                for stage, lag in stages:
                    stage(i if s >= lag else i - 1, (s - lag) % slots)
    for s in range(deepest):
        for stage, lag in stages:
            if s < lag:
                stage(turns - 1, s - lag + slots)


def first(it):
    return isinstance(it, int) and it == 0


def gnn_kernel(nc, x, src, dst, edge_attr_20, edge_weight, edge_weight_n2, w, out):
    ctx = ExitStack()
    with ctx:
        def sb(name, shape, dt=F32):
            return ctx.enter_context(nc.sbuf_tensor(name, shape, dt))

        def sem(name):
            return ctx.enter_context(nc.semaphore(name))

        def dram(name, shape):
            return nc.dram_tensor(name, shape, F32, kind="Internal").ap()

        slots_d = dram("slots_by_dst", (LANES * T, D_REC))
        slots_s = dram("slots_by_src", (LANES * T, S_REC))
        t_as = dram("table_src_score", (N, HEADS))
        t_h = dram("table_heads", (N, D))
        t_x1 = dram("table_x1", (N, D))
        t_fo = dram("table_feat_out", (N, D))
        t_fi = dram("table_feat_in", (N, D))
        t_g1 = dram("table_gat1", (N, G3 + 1))
        t_g2 = dram("table_gat2", (N, G3 + 1))
        d_aout = dram("spilled_a_out", (N, D))
        d_x = dram("spilled_x", (N, D))
        d_lat = dram("spilled_lat", (LAT, N))
        vd = slots_d.rearrange("(p t) c -> p t c", t=T)
        vs = slots_s.rearrange("(p t) c -> p t c", t=T)

        TABW = D + 2 * HEADS
        AR = T * (G3 + 1)
        arena = sb("arena", [LANES, AR])
        o_r0, o_x = 0, NT * TABW
        o_r1 = o_x + NT * D
        o_hg = o_r1 + NT * TABW
        o_msg = o_hg + SLOTS * TG * D
        o_apart = o_msg + 2 * TG * (D + HEADS)
        assert o_apart + TG * (RK + 2 * (RB + 1)) <= AR

        def view(off, rows, n):
            return arena[0:rows, off:off + n]

        acc0 = view(o_r0, P, NT * (D + HEADS)).rearrange("p (i f) -> p i f", f=D + HEADS)
        xs = view(o_x, P, NT * D).rearrange("p (i f) -> p i f", f=D)
        tab = view(o_r1, P, NT * TABW).rearrange("p (i f) -> p i f", f=TABW)
        as_e = view(o_r1, LANES, T * HEADS).rearrange("p (t h) -> p t h", h=HEADS)
        r0 = view(o_r0, P, NT * D).rearrange("p (i f) -> p i f", f=D)
        r1 = view(o_r1, P, NT * D).rearrange("p (i f) -> p i f", f=D)
        r0T = view(o_r0, LANES, 2 * N).rearrange("p (c n) -> p c n", c=2)
        r1T = view(o_r1, LANES, 2 * N).rearrange("p (c n) -> p c n", c=2)
        hg = view(o_hg, LANES, SLOTS * TG * D).rearrange("p (s j f) -> p s j f", s=SLOTS, j=TG)
        msg = view(o_msg, LANES, 2 * TG * (D + HEADS)).rearrange("p (s j f) -> p s j f", s=2, j=TG)
        keep3 = arena[:, :].rearrange("p (t f) -> p t f", f=G3 + 1)
        fio = view(o_hg, P, NSL * 2 * D).rearrange("p (s f) -> p s f", s=NSL)
        w_x2i = view(o_hg, LANES, 4 * 2 * D).rearrange("p (k m) -> p k m", k=4)
        w_h2h = view(o_hg + 8 * D, LANES, 2 * 2 * D).rearrange("p (k m) -> p k m", k=2)
        ai = view(o_msg, P, NSL * D).rearrange("p (s f) -> p s f", s=NSL)
        m1T, m2T, latT = view(o_r1, HID, N), view(o_r0, HID, N), view(o_r0 + N, LAT, N)

        def col(n, k=1):
            return view(n * EC, P, k * EC)

        aux_s = col(0, 4).rearrange("p (e c) -> p e c", c=4)
        aux_d = col(4, 4).rearrange("p (e c) -> p e c", c=4)
        hi = {"s": col(8), "d": col(9)}
        lo, mask, scan, rank, n_s, n_d, ew, ew2, adj = (col(10 + n) for n in range(9))
        assert 19 * EC <= o_hg

        o_up = [o_hg]

        def upper(rows, n):
            o_up[0] += n
            assert o_up[0] <= AR
            return view(o_up[0] - n, rows, n)

        FILL = T // 16
        fill_s = upper(LANES, FILL * S_REC).rearrange("p (t c) -> p t c", c=S_REC)
        fill_d = upper(LANES, FILL * D_REC).rearrange("p (t c) -> p t c", c=D_REC)
        group_i, group_f, bsum = upper(1, NG).bitcast(I32), upper(1, NG), upper(1, NG)
        pos = {"d": col(9), "s": upper(P, EC)}
        ints, ints2 = upper(P, EC).bitcast(I32), upper(P, EC).bitcast(I32)
        att = upper(LANES, 2 * D).rearrange("p (n f) -> p n f", n=2)
        att3 = upper(LANES, 4 * G3).rearrange("p (n f) -> p n f", n=4)
        wtmp = upper(LANES, D)
        wf1 = upper(RB + 1, 2 * D).rearrange("p (n f) -> p n f", n=2)

        iota_i = sb("iota_i", [LANES, LANES], I32)
        iota = sb("iota", [LANES, LANES])
        idn = sb("idn", [LANES, LANES])
        idnb = sb("idnb", [LANES, LANES], BF16)
        idn4 = sb("idn4", [LANES, HEADS, LANES], BF16)
        ones = sb("ones", [LANES, LANES])
        utri = sb("utri", [P, P])
        bkt = {"d": sb("bucket_d", [1, NG], I32), "s": sb("bucket_s", [1, NG], I32)}
        cnt, base = sb("cnt", [P, NT]), sb("base", [P, NT])
        tot_i, til_i = sb("tot_i", [LANES, NT], I32), sb("til_i", [LANES, NT], I32)
        til, ends, start = (sb(n, [LANES, NT]) for n in ("til", "ends", "start"))
        posi = sb("posi", [P, SSL, SC], I32)

        pay = sb("pay", [LANES, SLOTS, TG * S_REC])
        pay_d = pay[:, :, 0:TG * D_REC].rearrange("p s (j c) -> p s j c", c=D_REC)
        pay_s = pay[:, :, :].rearrange("p s (j c) -> p s j c", c=S_REC)
        idxi = sb("idxi", [LANES, SLOTS, TG], I32)
        oh = sb("onehot", [LANES, SLOTS, TG, P])
        ohb = sb("onehot_mask", [LANES, SLOTS, TG, P], BF16)
        turned_rows = sb("turned_rows", [LANES, 2, TG * LANES])
        ot = turned_rows[0:P, :, :].bitcast(BF16)[:, :, 0:TG * LANES].rearrange("p s (j e) -> p s j e", j=TG)
        rT = turned_rows[0:RK, :, :].bitcast(BF16)[:, :, 0:TG * LANES]
        apart = view(o_apart, LANES, TG * RK).bitcast(BF16)\
            .rearrange("p (s j q c) -> p s j q c", s=2, j=TG, q=len(A_PART))
        arest = view(o_apart + TG * RK, LANES, 2 * TG * (RB + 1)).rearrange("p (s j c) -> p s j c", s=2, j=TG)
        wide = sb("wide", [LANES, 4 * TG * LANES])
        hidT = wide[:, :].rearrange("p (s c e) -> p s c e", s=2, c=2)
        stage = wide[0:P, 0:SSL * SC * S_REC].rearrange("p (s e) -> p s e", s=SSL)
        gu = wide[:, 0:NSL * 2 * P].rearrange("p (s c n) -> p s c n", s=NSL, c=2)
        aT = wide[:, 0:12 * P].rearrange("p (b c n) -> p b c n", b=3, c=4)
        gT = wide[:, 12 * P:16 * P].rearrange("p (c n) -> p c n", c=4)
        A_BUF = (0, 1, 0, 1, 2)
        tm = sb("tm", [P, SLOTS, TG, HEADS])
        tm2 = sb("tm2", [P, SLOTS, HEADS])
        mx = sb("mx", [P, NT, HEADS])
        adm = sb("adm", [P, NT, 2 * HEADS])
        adm_rest = sb("adm_rest", [P, NT, 2 * HEADS])
        admp = sb("adm_parts", [P, NT, 3 * 2 * HEADS], BF16)
        admr = sb("adm_ring", [P, 2, 3 * 2 * HEADS], BF16)
        term = sb("dst_term", [LANES, 2, TG, 2 * HEADS])
        arg = sb("arg", [LANES, 2, TG, HEADS])
        hg3 = sb("hg3", [LANES, SLOTS, TG, G3 + 1])
        msg3 = sb("msg3", [LANES, 2, TG, G3 + 1])
        sum_ring = sb("sum_ring", [P, 2, G3 + 1])
        acc3 = sb("acc3", [P, NT, G3 + 1])
        tb3 = sb("tb3", [P, NT, G3 + 2])
        den = sb("den", [P, NT, HEADS])
        own = sb("own", [P, NT, HEADS])
        hs = sb("hs", [P, NSL, D])
        tT = sb("tT", [LANES, NSL, 2, P])
        onT = sb("onT", [LAT + 1, NSL, P])
        st = sb("st", [LANES, 2, NT, 6])
        lst = sb("lst", [P, NT, 6])
        lmean, lvar, lrstd, lnb = (sb(n, [P, NT]) for n in ("lmean", "lvar", "lrstd", "lnb"))
        mv, bsc, bsh = sb("mv", [LANES, 2, 2]), sb("bsc", [LANES, 2]), sb("bsh", [LANES, 2])
        ones3 = sb("ones3", [3, LANES], BF16)
        bparts, bf2p = sb("bparts", [1, 3, D], BF16), sb("bf2p", [3, D], BF16)
        brow = sb("brow", [1, 2, D])

        wx0 = sb("wx0", [LANES, 2, TABW])
        wf1p, wf1k = sb("wf1_parts", [RB + 1, 3, D], BF16), sb("wf1_stacked", [RK, D], BF16)
        wf2, wu1, wu2 = (sb(n, [LANES, 2, D]) for n in ("wf2", "wu1", "wu2"))
        wio = sb("wio", [LANES, 2, 2 * D])
        wm1, wg1 = sb("wm1", [LANES, 2, HID]), sb("wg1", [LANES, 2, G3 + 2])
        wm2, wm3 = sb("wm2", [HID, LANES]), sb("wm3", [HID, LANES])
        wg2, wgf, wf = sb("wg2", [G3, G3 + 2]), sb("wgf", [G3, LANES]), sb("wf", [LAT + 1, D])
        bias0, bias_io, bg = sb("bias0", [P, D]), sb("bias_io", [P, 2 * D]), sb("bg", [P, 2, G3])
        cols = sb("cols", [LANES, 16])
        cols3 = sb("cols3", [HID, 10])

        ps = [ctx.enter_context(nc.psum_tensor(f"ps{n}", [128, 512], F32)) for n in range(8)]

        def turned_at(sl, rows=LANES, banks=3):
            return ps[sl % banks][0:rows, 0:2 * P].rearrange("p (c n) -> p c n", c=2)

        def second_at(sl):
            return ps[2 + sl % 3]

        def third_at(sl):
            return ps[5 + sl % 3]

        PH = [
            dict(kind=MAX, order="d", heads=HEADS, width=HEADS, table=t_as, ring=hg3),
            dict(kind=SUM, order="d", heads=HEADS, width=D, table=t_h, ring=hg, acc=acc0),
            dict(kind=FILT, order="s", width=D, table=t_x1, ring=hg, acc=r0),
            dict(kind=WSUM, order="s", width=D, table=t_fo, ring=hg, acc=r1),
            dict(kind=WSUM, order="d", width=D, table=t_fi, ring=hg, acc=r1),
            dict(kind=MAX1, order="d", heads=1, width=G3 + 1, table=t_g1, ring=hg3),
            dict(kind=SUM, order="d", heads=1, width=G3, table=None, acc=acc3),
            dict(kind=MAX1, order="d", heads=1, width=G3 + 1, table=t_g2, ring=hg3),
            dict(kind=SUM, order="d", heads=1, width=G3, table=None, acc=acc3),
        ]
        ALL = (MAX, MAX1, SUM, FILT, WSUM)
        RATES = {
            "idx_ready": dict.fromkeys(ALL, 1),
            "onehot": dict.fromkeys(ALL, 1),
            "scattered": dict.fromkeys(ALL, 1) | {MAX: TG},
            "sums_copied": {SUM: 1},
            "acc_done": dict.fromkeys(ALL, 1),
            "reduced": {MAX: TG + 1, MAX1: 1},
            "kept": {MAX: 1, MAX1: 1},
            "attr_step": {FILT: 4},
            "turned": {SUM: 1, FILT: 1},
            "turn_copied": {SUM: 1, FILT: 1},
            "parts_ready": {SUM: 1},
            "dst_terms": {SUM: 1},
            "score_step": {SUM: 5},
            "exp_ready": {SUM: 1},
            "msg_ready": {SUM: 1, FILT: 2},
            "hidden": {FILT: 1},
            "hidden_act": {FILT: 1},
            "filtered": {FILT: 2},
        }
        esem = {n: sem(n) for n in RATES}
        loaded = [sem(f"loaded{s}") for s in range(SLOTS)]
        gathered = [sem(f"gathered{s}") for s in range(SLOTS)]

        by_table = {"idx_ready": True, "sums_copied": False}

        def before(k, name):
            return sum(NG * RATES[name].get(p["kind"], 0) for p in PH[:k]
                       if name not in by_table or by_table[name] == (p["table"] is not None))

        def gathers_before(k):
            return 16 * TG * NI * sum(p["table"] is not None for p in PH[:k])

        def wait_for(eng, k, name, it, sl, c=0, back=0):
            if sl < back:
                if first(it):
                    return
                it, sl = it - 1, sl + SLOTS
            r = RATES[name][PH[k]["kind"]]
            eng.wait_ge(esem[name], before(k, name) + r * SLOTS * it + r * (sl - back) + (c or r))

        def wait_loaded(eng, k, it, sl):
            eng.wait_ge(loaded[sl], 16 * NI * k + 16 * (it + 1))

        def wait_gathered(eng, k, it, sl):
            eng.wait_ge(gathered[sl], gathers_before(k) + 16 * TG * (it + 1))

        def phase_begins(eng, k):
            if k:
                eng.wait_ge(esem["acc_done"], before(k, "acc_done"))
                eng.wait_ge(esem["kept"], before(k, "kept"))

        def sum_at(k, sl):
            ph = PH[k]
            return ps[sl % (2 if ph["kind"] == FILT else 4)][
                0:P, 0:ph["width"] + (ph["heads"] if ph["kind"] == SUM else 0)]

        def sum_banks(k):
            return 2 if PH[k]["kind"] == FILT else 4

        s = {n: sem(n) for n in """consts consts_v w_small in_edges in_x filled blank w_late ln_stats link sort_step sort_go
             cnt_ready prefix_ready stage_cp sorted_d sorted_s att_ready table_ready table_spare spill lat_in
             pool_go sp_go parts_in""".split()}
        st_ld = [sem(f"st_ld{n}") for n in range(SSL)]
        scat = [sem(f"scat{n}") for n in range(SSL)]
        SCAT1 = 16 * SC * (NSS // SSL)
        NODE = dict(a=(0, 1, 2, 3, 5), t=(0, 2, 3, 4, 5, 8, 9), c=(0, 2, 3, 4, 5, 8, 9), m=(0, 3, 5, 6, 7, 8, 9),
                    o=(0, 8, 9), p=(2,), b=(2, 5, 6, 7, 9), q=(2, 8, 9), y=(2, 4, 9), j=(2, 3, 5, 6, 7),
                    h=(2, 3), g=(2, 4, 5), e=(2,), v=(3,), f=(3, 9), i=(4,), x=(4,), d=(4,), z=(4,), w=(9,))
        NODE_RATE = {"d4": 3, "f9": 2}
        node = {letter: sem(f"node_{letter}") for letter in NODE}
        slot_sem = {}

        def nsem(name):
            if name[1:].isdigit():
                assert int(name[1:]) in NODE[name[0]], name
                return node[name[0]]
            if name not in slot_sem:
                slot_sem[name] = sem(name)
            return slot_sem[name]

        def nbase(name):
            return sum(NT * NODE_RATE.get(f"{name[0]}{k}", 1) for k in NODE[name[0]] if k < int(name[1:]))

        def nwait(eng, name, it, sl, back=0, c=0):
            if sl < back:
                if first(it):
                    return
                it, sl = it - 1, sl + NSL
            r = NODE_RATE.get(name, 1)
            eng.wait_ge(nsem(name), nbase(name) + r * NSL * it + r * (sl - back) + (c or r))

        def all_tiles(eng, name):
            eng.wait_ge(nsem(name), nbase(name) + NT * NODE_RATE.get(name, 1))

        NORMS = ("ln0", "ln1", "bn1", "ln2", "bn2", "ln3", "bn5", "bn6", "bn7")
        ONCE = {"variance": NORMS, "deviation": NORMS, "norm": NORMS, "relu": ("r5", "r6", "r7"),
                "maxima": ("adm0", "adm5", "adm7"),
                "sums_begun": ("acc6", "acc8"),
                "own_weight": ("adm0", "adm5", "adm7"), "attended": ("fin8", "fin9"), "taken": ("h0", "x1")}
        once = {kind: sem(kind) for kind in ONCE}

        def wait_once(eng, kind, name):
            eng.wait_ge(once[kind], ONCE[kind].index(name) + 1)

        def tiles(eng, *stages):
            skewed(eng, NNI, NSL, stages)

        def rows_of(i):
            return bass.ds(P * i, P)

        def flat(ap):
            return ap.rearrange("p a f -> p (a f)")

        def tile_no(it, sl):
            return NSL * it + sl

        def by_node(ap):
            return ap.rearrange("(i p) f -> p i f", p=P)

        W_LOADS = []

        def wload(to, frm):
            W_LOADS.append((to, frm))

        for c in range(2):
            a, b = c * LANES, (c + 1) * LANES
            wload(wx0[:, c, 0:D].rearrange("p (h f) -> p h f", h=HEADS),
                  w["L0_gnn_W"][:, a:b, :].rearrange("h p f -> p h f"))
            for to, name in ((wf2, "L1_gnn_Wf2"), (wu1, "L1_gnn_Wu1"), (wu2, "L1_gnn_Wu2"),
                             (wm1, "L3_gnn_W_m1")):
                wload(to[:, c, :], w[name][a:b, :])
            wload(wio[:, c, 0:D], w["L2_gnn_W_in"][a:b, :])
            wload(wio[:, c, D:2 * D], w["L2_gnn_W_out"][a:b, :])
            wload(wg1[:, c, 0:G3], w["L3_gnn_W_g1"][a:b, :])
        wload(wf1[0:RB, 0, :], w["L1_gnn_Wf1"])
        wload(wf1[RB:RB + 1, 0, :], w["L1_gnn_bf1"].unsqueeze(0))
        wload(brow[:, 0, :], w["L1_gnn_bf2"].unsqueeze(0))
        wload(att[:, 0, :], w["L0_gnn_att_src"].rearrange("h f -> (h f)").partition_broadcast(LANES))
        wload(att[:, 1, :], w["L0_gnn_att_dst"].rearrange("h f -> (h f)").partition_broadcast(LANES))
        for n, name in enumerate(["as_g1", "ad_g1", "as_g2", "ad_g2"]):
            wload(att3[:, n, :], w[f"L3_gnn_{name}"].partition_broadcast(LANES))
        wload(bias0[:, :], w["L0_gnn_bias"].partition_broadcast(P))
        wload(bias_io[:, 0:D], w["L2_gnn_b_in"].partition_broadcast(P))
        wload(bias_io[:, D:2 * D], w["L2_gnn_b_out"].partition_broadcast(P))
        wload(bg[:, 0, :], w["L3_gnn_b_g1"].partition_broadcast(P))
        wload(bg[:, 1, :], w["L3_gnn_b_g2"].partition_broadcast(P))
        wload(wm2[:, 0:HID], w["L3_gnn_W_m2"])
        wload(wm3[:, 0:LAT], w["L3_gnn_W_m3"])
        wload(wg2[:, 0:G3], w["L3_gnn_W_g2"])
        wload(wgf[:, 0:LAT], w["L3_gnn_W_gf"])
        wload(wf[0:LAT, :], w["L3_gnn_W_f"])
        wload(wf[LAT:LAT + 1, :], w["L3_gnn_b_f"].unsqueeze(0))
        for n, name in enumerate(["L1_gnn_bu1", "L1_gnn_bu2", "L1_gnn_gamma", "L1_gnn_beta",
                                  "L2_gnn_gamma", "L2_gnn_beta"]):
            for c in range(2):
                wload(cols[:, 2 * n + c:2 * n + c + 1], w[name][c * LANES:(c + 1) * LANES].unsqueeze(1))
        for c in range(4):
            wload(cols[:, 12 + c:13 + c], w["L2_gnn_b_x2i"][c * LANES:(c + 1) * LANES].unsqueeze(1))
        for n, name in enumerate(["b_m1", "g_m1", "be_m1", "b_m2", "g_m2", "be_m2"]):
            wload(cols3[:, n:n + 1], w[f"L3_gnn_{name}"].unsqueeze(1))
        for n, name in enumerate(["b_m3", "g_m3", "be_m3", "b_gf"]):
            wload(cols3[0:LAT, 6 + n:7 + n], w[f"L3_gnn_{name}"].unsqueeze(1))

        block = ctx.enter_context(nc.Block())

        @block.sync
        def _(sp):
            for to, frm in ((ints, dst), (ints2, src), (ew, edge_weight), (ew2, edge_weight_n2)):
                sp.dma_start(to, frm.rearrange("(p e) -> p e", e=EC)).then_inc(s["in_edges"], 16)
            sp.wait_ge(s["filled"], 1)
            for n in range(T // FILL):
                sp.dma_start(vd[:, n * FILL:(n + 1) * FILL, :], fill_d).then_inc(s["blank"], 16)
                sp.dma_start(vs[:, n * FILL:(n + 1) * FILL, :], fill_s).then_inc(s["blank"], 16)
            for to, frm in W_LOADS:
                sp.dma_start(to, frm).then_inc(s["w_small"], 16)

            av = edge_attr_20.rearrange("(p e) c -> p e c", e=EC)

            def attr(it, sl):
                sp.wait_ge(scat[sl], SCAT1 + 16 * SC * it)
                sp.sem_inc(s["sp_go"], 1)
                sp.dma_start(stage[:, sl, :].rearrange("p (e c) -> p e c", c=S_REC)[:, :, 0:RB],
                             av[:, bass.ds(SSL * SC * it + SC * sl, SC), :]).then_inc(st_ld[sl], 16)
            def attr_turns(begin, end):
                with sp.Fori(begin, end) as it:
                    for sl in range(SSL):
                        attr(it, sl)

            sp.wait_ge(s["sorted_s"], 1)
            sp.wait_ge(s["stage_cp"], NSS)
            sp.dma_start(xs, by_node(x)).then_inc(s["in_x"], 16)
            attr_turns(0, S_NODES)

            def edge_loads(k):
                ph = PH[k]
                phase_begins(sp, k)

                def load(it, sl):
                    wait_for(sp, k, "onehot", it, sl, back=SLOTS)
                    sp.sem_inc(s["sp_go"], 1)
                    if ph["table"] is not None:
                        wait_for(sp, k, "idx_ready", it, sl, back=SLOTS)
                        sp.sem_inc(s["sp_go"], 1)
                    if ph["kind"] == FILT:
                        wait_for(sp, k, "attr_step", it, sl, c=2, back=SLOTS)
                        sp.sem_inc(s["sp_go"], 1)
                    to, frm = (pay_d, vd) if ph["order"] == "d" else (pay_s, vs)
                    sp.dma_start(to[:, sl, :, :], frm[:, bass.ds(TG * SLOTS * it + TG * sl, TG), :])\
                      .then_inc(loaded[sl], 16)
                skewed(sp, NI, SLOTS, [(load, 0)])

            all_tiles(sp, "o0")
            sp.dma_start(by_node(t_h), tab[:, :, 0:D]).then_inc(s["table_ready"], 16)
            sp.dma_start(by_node(t_as), tab[:, :, D:D + HEADS]).then_inc(s["table_ready"], 16)
            attr_turns(S_NODES, NSS // SSL)
            sp.wait_ge(s["att_ready"], 1)
            for n in range(3):
                sp.dma_start(bf2p[n:n + 1, :], bparts[:, n, :]).then_inc(s["parts_in"], 16)
            for n, part in enumerate(W_PART):
                sp.dma_start(wf1k[n * (RB + 1):(n + 1) * (RB + 1), :], wf1p[:, part, :]).then_inc(s["parts_in"], 16)
            edge_loads(0)
            edge_loads(1)
            for sl in range(SSL):
                sp.wait_ge(scat[sl], 2 * SCAT1)
            all_tiles(sp, "a1")
            sp.dma_start(by_node(t_x1), r1).then_inc(s["table_ready"], 16)
            edge_loads(2)

            def feat(it, sl):
                nwait(sp, "f3", it, sl)
                sp.sem_inc(s["sp_go"], 1)
                i = tile_no(it, sl)
                sp.dma_start(t_fi[rows_of(i), :], fio[:, sl, 0:D]).then_inc(nsem(f"k3_{sl}"), 16)
                sp.dma_start(t_fo[rows_of(i), :], fio[:, sl, D:2 * D]).then_inc(nsem(f"k3_{sl}"), 16)
            tiles(sp, (feat, 0))
            edge_loads(3)
            sp.wait_ge(esem["acc_done"], before(4, "acc_done"))
            sp.dma_start(by_node(d_aout), r1).then_inc(s["spill"], 16)
            edge_loads(4)
            sp.wait_ge(esem["acc_done"], before(5, "acc_done"))
            sp.dma_start(w_x2i, w["L2_gnn_W_x2i"].rearrange("(k p) m -> p k m", p=LANES))\
              .then_inc(s["w_late"], 16)
            sp.dma_start(w_h2h, w["L2_gnn_W_h2h"].rearrange("(k p) m -> p k m", p=LANES))\
              .then_inc(s["w_late"], 16)

            def a_out(it, sl):
                nwait(sp, "t4", it, sl, back=NSL)
                sp.sem_inc(s["sp_go"], 1)
                sp.dma_start(hs[:, sl, :], d_aout[rows_of(tile_no(it, sl)), :]).then_inc(nsem(f"ld4_{sl}"), 16)
            sp.wait_ge(s["spill"], 16)
            tiles(sp, (a_out, 0))
            all_tiles(sp, "y4")
            sp.dma_start(by_node(d_x), xs).then_inc(s["spill"], 16)
            all_tiles(sp, "g5")
            sp.dma_start(by_node(t_g1), tb3[:, :, 0:G3 + 1]).then_inc(s["table_ready"], 16)
            wait_once(sp, "relu", "r7")
            sp.dma_start(d_lat, latT).then_inc(s["spill"], 16)
            edge_loads(5)
            edge_loads(6)
            all_tiles(sp, "o8")
            sp.dma_start(by_node(t_g2), tb3[:, :, 0:G3 + 1]).then_inc(s["table_ready"], 16)
            edge_loads(7)
            edge_loads(8)

            def x_back(it, sl):
                if not first(it):
                    sp.wait_ge(nsem(f"st9_{sl}"), 16 * it)
                    sp.sem_inc(s["sp_go"], 1)
                sp.dma_start(r1[:, sl, :], d_x[rows_of(tile_no(it, sl)), :]).then_inc(nsem(f"ld9_{sl}"), 16)

            def store(it, sl):
                nwait(sp, "y9", it, sl)
                sp.sem_inc(s["sp_go"], 1)
                sp.dma_start(out[rows_of(tile_no(it, sl)), :], r1[:, sl, :]).then_inc(nsem(f"st9_{sl}"), 16)
            sp.wait_ge(esem["acc_done"], before(9, "acc_done"))
            sp.dma_start(latT, d_lat).then_inc(s["lat_in"], 16)
            tiles(sp, (x_back, 0), (store, 3))
            for sl in range(NSL):
                sp.wait_ge(nsem(f"st9_{sl}"), 16 * NNI)

        @block.gpsimd
        def _(pool):
            nc.gpsimd.memset(fill_s, 0.0)
            nc.gpsimd.memset(fill_d, 0.0).then_inc(s["pool_go"], 1)
            pool.wait_ge(s["pool_go"], 1)
            nc.gpsimd.memset(fill_s[:, :, S_LO], -1.0)
            nc.gpsimd.memset(fill_d[:, :, D_LO], -1.0).then_inc(s["filled"], 1)
            nc.gpsimd.iota(iota_i[:, :], pattern=[[1, LANES]], base=0, channel_multiplier=0)
            nc.gpsimd.iota(group_i, pattern=[[1, NG]], base=0, channel_multiplier=0)
            nc.gpsimd.memset(idn[:, :], 0.0)
            nc.gpsimd.memset(utri[:, :], 0.0)
            nc.gpsimd.memset(ones[:, :], 1.0).then_inc(s["consts"], 1)
            pool.wait_ge(s["consts"], 1)
            nc.gpsimd.affine_select(out=idn[:, :], in_=idn[:, :], compare_op=ALU.not_equal, fill=1.0,
                                    base=0, pattern=[[-1, LANES]], channel_multiplier=1).then_inc(s["consts"], 1)
            nc.gpsimd.affine_select(out=utri[:, :], in_=utri[:, :], compare_op=ALU.is_ge, fill=1.0,
                                    base=0, pattern=[[-1, P]], channel_multiplier=1).then_inc(s["consts"], 1)

            def scatter_step(order, rec, dest):
                n0 = 0 if order == "d" else NSS

                def step(it, sl):
                    pool.wait_ge(s["stage_cp"], n0 + SSL * it + sl + 1)
                    pool.sem_inc(s["pool_go"], 1)
                    if order == "s":
                        pool.wait_ge(st_ld[sl], 16 * (it + 1))
                        pool.sem_inc(s["pool_go"], 1)
                    for c in range(SC):
                        pool.indirect_dma_start(
                            dest, bass.IndirectOffsetOnAxis(ap=posi[:, sl, c:c + 1], axis=0),
                            stage[:, sl, c * rec:(c + 1) * rec], None).then_inc(scat[sl], 16)
                return step

            pool.wait_ge(s["blank"], 2 * 16 * (T // FILL))
            skewed(pool, NSS // SSL, SSL, [(scatter_step("d", D_REC, slots_d), 0)])
            scatter_s = scatter_step("s", S_REC, slots_s)
            skewed(pool, NSS // SSL - 1, SSL, [(scatter_s, 0)])

            def gathers(k):
                ph = PH[k]
                phase_begins(pool, k)

                def step(it, sl):
                    wait_for(pool, k, "idx_ready", it, sl)
                    pool.sem_inc(s["pool_go"], 1)
                    if not first(it):
                        if ph["kind"] in (MAX, MAX1):
                            wait_for(pool, k, "kept", it, sl, back=SLOTS)
                            pool.sem_inc(s["pool_go"], 1)
                        wait_for(pool, k, "scattered" if ph["kind"] in (MAX, MAX1, WSUM) else "msg_ready",
                                 it, sl, back=SLOTS)
                        pool.sem_inc(s["pool_go"], 1)
                    for j in range(TG):
                        pool.indirect_dma_start(
                            ph["ring"][:, sl, j, 0:ph["width"]], None, ph["table"],
                            bass.IndirectOffsetOnAxis(ap=idxi[:, sl, j:j + 1], axis=0))\
                            .then_inc(gathered[sl], 16)
                skewed(pool, NI, SLOTS, [(step, 0)])

            pool.wait_ge(s["table_ready"], 32)
            gathers(0)
            gathers(1)
            for sl in range(SSL):
                scatter_s(NSS // SSL - 1, sl)
            pool.wait_ge(s["table_ready"], 48)
            gathers(2)
            for sl in range(NSL):
                pool.wait_ge(nsem(f"k3_{sl}"), 32 * NNI)
            gathers(3)
            gathers(4)
            pool.wait_ge(s["table_ready"], 64)
            gathers(5)

            def sum_up(k):
                phase_begins(pool, k)
                wait_once(pool, "sums_begun", f"acc{k}")

                def step(it, sl):
                    b = pool.value_load(bkt["d"][0:1, bass.ds(SLOTS * it + sl, 1)], min_val=0, max_val=NT - 1)
                    wait_for(pool, k, "sums_copied", it, sl)
                    pool.sem_inc(s["pool_go"], 1)
                    wait_for(pool, k, "acc_done", it, sl, back=1)
                    pool.sem_inc(s["pool_go"], 1)
                    a = flat(acc3[:, bass.ds(b, 1), :])
                    nc.gpsimd.tensor_tensor(a, a, sum_ring[:, sl % 2, :], ALU.add).then_inc(esem["acc_done"], 1)
                skewed(pool, NI, SLOTS, [(step, 0)])

            sum_up(6)
            pool.wait_ge(s["table_ready"], 80)
            gathers(7)
            sum_up(8)

        @block.scalar
        def _(act):
            A = nc.scalar.activation

            def stage_step(order):
                aux, rec, off = (aux_d, D_REC, 0) if order == "d" else (aux_s, S_REC, RB)
                done = 0 if order == "d" else SCAT1
                act.wait_ge(s["sorted_" + order], 1)

                def step(it, sl):
                    if done or not first(it):
                        act.wait_ge(scat[sl], done + 16 * SC * it)
                    span = bass.ds(SSL * SC * it + SC * sl, SC)
                    A(stage[:, sl, 0:SC * rec].rearrange("p (e c) -> p e c", c=rec)[:, :, off:off + 4],
                      aux[:, span, :], ACT.Copy)
                    A(posi[:, sl, :], pos[order][:, span], ACT.Copy).then_inc(s["stage_cp"], 1)
                return step

            skewed(act, NSS // SSL, SSL, [(stage_step("d"), 0)])
            step_s = stage_step("s")
            for sl in range(SSL):
                step_s(0, sl)

            def normalised(it, sl, to):
                i = tile_no(it, sl)
                return A(to, flat(xs[:, bass.ds(i, 1), :]), ACT.Relu,
                         bias=lnb[:, bass.ds(i, 1)], scale=lrstd[:, bass.ds(i, 1)])

            def to_ring(name, freed_by):
                def stage_(it, sl):
                    nwait(act, freed_by, it, sl, back=NSL)
                    normalised(it, sl, hs[:, sl, :]).then_inc(nsem(name), 1)
                return stage_

            def norm_ready(name, ap):
                wait_once(act, "variance", name)
                A(ap, ap, ACT.Sqrt).then_inc(once["deviation"], 1)
                wait_once(act, "norm", name)

            def own_weight(H, name):
                wait_once(act, "maxima", name)
                A(own[:, :, 0:H], own[:, :, 0:H], ACT.Exp).then_inc(once["own_weight"], 1)

            def table0(it, sl):
                nwait(act, "m0", it, sl)
                A(flat(tab[:, bass.ds(tile_no(it, sl), 1), :]), ps[3 + sl][0:P, 0:TABW], ACT.Copy)\
                    .then_inc(nsem("o0"), 1)
            norm_ready("ln0", lrstd[:, :])
            tiles(act, (to_ring("a0", "t0"), 0), (table0, 3))
            with act.Fori(1, NSS // SSL) as it:
                for sl in range(SSL):
                    step_s(it, sl)

            def edges(k):
                ph = PH[k]
                kind, H, width = ph["kind"], ph.get("heads"), ph["width"]
                phase_begins(act, k)

                def indices(it, sl):
                    wait_loaded(act, k, it, sl)
                    if not first(it):
                        act.wait_ge(gathered[sl], gathers_before(k) + 16 * TG * it)
                    A(idxi[:, sl, :], pay_d[:, sl, :, D_IDX] if ph["order"] == "d" else pay_s[:, sl, :, S_IDX],
                      ACT.Copy).then_inc(esem["idx_ready"], 1)

                def keep(it, sl):
                    wait_gathered(act, k, it, sl)
                    to = as_e if H == HEADS else keep3
                    A(to[:, bass.ds(TG * SLOTS * it + TG * sl, TG), :], hg3[:, sl, :, 0:width], ACT.Copy)\
                        .then_inc(esem["kept"], 1)

                def parts(it, sl):
                    b = act.value_load(bkt[ph["order"]][0:1, bass.ds(SLOTS * it + sl, 1)],
                                       min_val=0, max_val=NT - 1)
                    wait_for(act, k, "dst_terms", it, sl, back=2)
                    A(admr[:, sl % 2, 0:6 * H], flat(admp[:, bass.ds(b, 1), 0:6 * H]), ACT.Copy)\
                        .then_inc(esem["parts_ready"], 1)

                def turn_copy(it, sl):
                    wait_for(act, k, "turned", it, sl)
                    if kind == SUM:
                        wait_for(act, k, "dst_terms", it, sl, back=2)
                        A(ot[:, sl % 2, :, :], ps[4 + sl % 2][0:P, :].rearrange("p (j e) -> p j e", j=TG),
                          ACT.Copy).then_inc(esem["turn_copied"], 1)
                    else:
                        wait_for(act, k, "hidden", it, sl, back=2)
                        A(rT[:, sl % 2, :], ps[4][0:RK, :], ACT.Copy).then_inc(esem["turn_copied"], 1)

                def exps(it, sl):
                    wait_for(act, k, "score_step", it, sl)
                    wait_for(act, k, "scattered", it, sl, back=2)
                    A((msg if H == HEADS else msg3)[:, sl % 2, :, width:width + H], arg[:, sl % 2, :, 0:H],
                      ACT.Exp).then_inc(esem["exp_ready"], 1)

                def copy_sums(it, sl):
                    wait_for(act, k, "scattered", it, sl)
                    wait_for(act, k, "acc_done", it, sl, back=2)
                    A(sum_ring[:, sl % 2, :], sum_at(k, sl), ACT.Copy).then_inc(esem["sums_copied"], 1)

                def silu(it, sl):
                    wait_for(act, k, "hidden", it, sl)
                    wait_for(act, k, "filtered", it, sl, back=2)
                    A(hidT[:, sl % 2, 0, :], ps[5][:, :], ACT.Silu)
                    A(hidT[:, sl % 2, 1, :], ps[6][:, :], ACT.Silu).then_inc(esem["hidden_act"], 1)

                stages = [(indices, 0)] if ph["table"] is not None else [(copy_sums, 3)]
                stages += {MAX: [(keep, 3)], MAX1: [(keep, 3)], SUM: [(parts, 0), (turn_copy, 0), (exps, 1)],
                           FILT: [(silu, 1), (turn_copy, 0)], WSUM: []}[kind]
                skewed(act, NI, SLOTS, stages)

            act.wait_ge(s["table_ready"], 32)
            wait_once(act, "taken", "h0")
            edges(0)
            own_weight(HEADS, "adm0")
            edges(1)

            def h1(it, sl):
                normalised(it, sl, flat(r1[:, bass.ds(tile_no(it, sl), 1), :])).then_inc(nsem("a1"), 1)
            norm_ready("ln1", lrstd[:, :])
            tiles(act, (h1, 0))
            edges(2)

            def agg(it, sl):
                nwait(act, "t2", it, sl, back=NSL)
                A(hs[:, sl, :], flat(r0[:, bass.ds(tile_no(it, sl), 1), :]), ACT.Copy).then_inc(nsem("a2"), 1)

            def silu_u(it, sl):
                nwait(act, "p2", it, sl)
                nwait(act, "q2", it, sl, back=NSL)
                A(gu[:, sl, 0, :], second_at(sl)[:, 0:P], ACT.Silu, bias=cols[:, 0:1])
                A(gu[:, sl, 1, :], second_at(sl)[:, P:2 * P], ACT.Silu, bias=cols[:, 1:2]).then_inc(nsem("b2"), 1)

            def bias_u(it, sl):
                nwait(act, "q2", it, sl)
                for c in range(2):
                    last = A(r1T[:, c, rows_of(tile_no(it, sl))], third_at(sl)[:, c * P:(c + 1) * P], ACT.Identity,
                             bias=cols[:, 2 + c:3 + c])
                last.then_inc(nsem("y2"), 1)
            act.wait_ge(esem["acc_done"], before(3, "acc_done"))
            wait_once(act, "taken", "x1")
            act.wait_ge(s["table_ready"], 48)
            tiles(act, (agg, 0), (silu_u, 2), (bias_u, 3))

            def affine(name, source, freed_by):
                def stage_(it, sl):
                    for f in freed_by:
                        nwait(act, f, it, sl, back=NSL)
                    for c in range(2):
                        last = A(tT[:, sl, c, :], source[:, c, rows_of(tile_no(it, sl))], ACT.Identity,
                                 bias=bsh[:, c:c + 1], scale=bsc[:, c:c + 1])
                    last.then_inc(nsem(name), 1)
                return stage_
            norm_ready("bn1", bsc[:, :])
            tiles(act, (affine("h2", r1T, ["g2"]), 0))

            norm_ready("ln2", lrstd[:, :])
            tiles(act, (to_ring("a3", "t3"), 0))
            norm_ready("bn2", bsc[:, :])
            tiles(act, (affine("h3", r0T, ["m3", "v3"]), 0))
            edges(3)
            edges(4)

            def a_in(it, sl):
                nwait(act, "t4", it, sl, back=NSL)
                A(ai[:, sl, :], flat(r1[:, bass.ds(tile_no(it, sl), 1), :]), ACT.Copy).then_inc(nsem("i4"), 1)

            def a_turned(it, sl):
                nwait(act, "t4", it, sl)
                nwait(act, "x4", it, sl, back=2)
                A(aT[:, A_BUF[sl], :, :].rearrange("p c n -> p (c n)"), ps[0][:, 0:4 * P], ACT.Copy).then_inc(nsem("c4"), 1)

            def gates(it, sl):
                nwait(act, "x4", it, sl)
                nwait(act, "d4", it, sl, back=1)
                for c in range(4):
                    last = A(gT[:, c, :], ps[3 + sl][:, c * P:(c + 1) * P], ACT.Sigmoid if c < 2 else ACT.Tanh,
                             bias=cols[:, 12 + c:13 + c])
                last.then_inc(nsem("g4"), 1)
            act.wait_ge(esem["acc_done"], before(5, "acc_done"))
            tiles(act, (a_in, 0), (a_turned, 1), (gates, 2))

            def bias_stage(name, got, to, frm, bias):
                def stage_(it, sl):
                    nwait(act, got, it, sl)
                    A(to[:, rows_of(tile_no(it, sl))], frm(sl), ACT.Identity, bias=bias).then_inc(nsem(name), 1)
                return stage_

            def norm_relu(n, to, rows):
                norm_ready(f"bn{n}", bsc[0:rows, 0:1])
                A(to, to, ACT.Relu, bias=bsh[0:rows, 0:1], scale=bsc[0:rows, 0:1]).then_inc(once["relu"], 1)

            norm_ready("ln3", lrstd[:, :])
            tiles(act, (to_ring("a5", "t5"), 0),
                  (bias_stage("b5", "m5", m1T, lambda sl: third_at(sl)[0:HID, 0:P], cols3[:, 0:1]), 2))
            norm_relu(5, m1T, HID)
            tiles(act, (bias_stage("b6", "m6", m2T, lambda sl: ps[sl][0:HID, 0:P], cols3[:, 3:4]), 0))
            norm_relu(6, m2T, HID)
            tiles(act, (bias_stage("b7", "m7", latT, lambda sl: ps[sl][0:LAT, 0:P], cols3[0:LAT, 6:7]), 0))
            norm_relu(7, latT, LAT)

            def relu_out(name, freed_by):
                def stage_(it, sl):
                    nwait(act, freed_by, it, sl, back=NSL)
                    A(hs[:, sl, 0:G3], flat(acc3[:, bass.ds(tile_no(it, sl), 1), 0:G3]), ACT.Relu)\
                        .then_inc(nsem(name), 1)
                return stage_
            act.wait_ge(s["spill"], 48)
            edges(5)
            own_weight(1, "adm5")
            edges(6)
            wait_once(act, "attended", "fin8")
            tiles(act, (relu_out("q8", "t8"), 0))
            edges(7)
            own_weight(1, "adm7")
            edges(8)

            def gf_bias(it, sl):
                nwait(act, "m9", it, sl)
                nwait(act, "f9", it, sl, back=NSL)
                A(tT[0:LAT, sl, 1, :], ps[3 + sl][0:LAT, 256:256 + P], ACT.Identity, bias=cols3[0:LAT, 9:10])\
                    .then_inc(nsem("b9"), 1)

            def out_relu(it, sl):
                nwait(act, "o9", it, sl)
                A(hs[:, sl, :], ps[3 + sl][0:P, 0:D], ACT.Relu).then_inc(nsem("w9"), 1)
            wait_once(act, "attended", "fin9")
            tiles(act, (relu_out("q9", "y9"), 0), (gf_bias, 2), (out_relu, 3))

        @block.tensor
        def _(pe):
            MM = nc.tensor.matmul

            pe.wait_ge(s["consts"], 3)
            for n in range(2):
                pe.wait_ge(s["cnt_ready"], n + 1)
                MM(ps[0][0:P, 0:NT], utri[:, :], cnt[:, :], start=True, stop=True)
                MM(ps[0][:, 64:64 + NT], ones[0:P, :], cnt[:, :], start=True, stop=True)\
                    .then_inc(s["prefix_ready"], 1)

            def turn(name, got, freed_by, rows=2 * LANES, banks=3):
                def stage_(it, sl):
                    nwait(pe, got, it, sl)
                    nwait(pe, freed_by, it, sl, back=banks - 1)
                    if rows == G3:
                        last = nc.tensor.transpose(turned_at(sl, G3, banks)[:, 0, :], hs[:, sl, 0:G3], idn[0:P, 0:P])
                    else:
                        for c in range(2):
                            last = nc.tensor.transpose(turned_at(sl, LANES, banks)[:, c, :], hs[:, sl, c * LANES:(c + 1) * LANES],
                                                       idn[0:P, 0:P])
                    last.then_inc(nsem(name), 1)
                return stage_

            def table(name, got, freed_by, wide_w, width):
                def stage_(it, sl):
                    nwait(pe, got, it, sl)
                    nwait(pe, freed_by, it, sl, back=NSL)
                    for c in range(2):
                        last = MM(ps[3 + sl][0:P, 0:width], tT[:, sl, c, :], wide_w[:, c, :],
                                  start=(c == 0), stop=(c == 1))
                    last.then_inc(nsem(name), 1)
                return stage_

            pe.wait_ge(s["w_small"], 16 * len(W_LOADS))
            pe.wait_ge(s["att_ready"], 1)
            tiles(pe, (turn("t0", "a0", "c0"), 0), (table("m0", "c0", "o0", wx0, TABW), 1))

            def edges(k):
                ph = PH[k]
                kind, H, width = ph["kind"], ph.get("heads"), ph["width"]
                total = width + (H if kind == SUM else 0)
                phase_begins(pe, k)

                def maxima(it, sl):
                    wait_for(pe, k, "onehot", it, sl)
                    wait_gathered(pe, k, it, sl)
                    if kind == MAX1:
                        wait_for(pe, k, "reduced", it, sl, back=SLOTS)
                    for j in range(TG):
                        if kind == MAX:
                            wait_for(pe, k, "reduced", it, sl, c=j + 1, back=1)
                        to = ps[j if kind == MAX else sl][0:P, :]
                        c0 = 0 if kind == MAX else j * LANES
                        MM(to[:, c0:c0 + H * LANES], ohb[:, sl, j, :],
                           idn4[:, 0:H, :].rearrange("p h e -> p (h e)"), start=True, stop=False)
                        for h in range(H):
                            a = width - H + h
                            last = MM(to[:, c0 + h * LANES:c0 + (h + 1) * LANES],
                                      hg3[:, sl, j, a:a + 1].to_broadcast([LANES, P]), idn[:, :],
                                      start=False, stop=(h == H - 1))
                        if kind == MAX or j == TG - 1:
                            last.then_inc(esem["scattered"], 1)

                def turn_onehot(it, sl):
                    wait_for(pe, k, "onehot", it, sl)
                    wait_for(pe, k, "turn_copied", it, sl, back=2)
                    for j in range(TG):
                        last = nc.tensor.transpose(ps[4 + sl % 2][0:P, j * LANES:(j + 1) * LANES],
                                                   oh[:, sl, j, :], idn[:, :])
                    last.then_inc(esem["turned"], 1)

                def dst_terms(it, sl):
                    wait_for(pe, k, "turn_copied", it, sl)
                    wait_for(pe, k, "score_step", it, sl, c=1, back=2)
                    wait_for(pe, k, "parts_ready", it, sl)
                    for j in range(TG):
                        last = MM(ps[6 + sl % 2][:, 6 * H * j:6 * H * (j + 1)], ot[:, sl % 2, j, :],
                                  admr[:, sl % 2, 0:6 * H], start=True, stop=True)
                    last.then_inc(esem["dst_terms"], 1)

                def sums(it, sl):
                    if kind == WSUM:
                        wait_for(pe, k, "onehot", it, sl)
                        wait_gathered(pe, k, it, sl)
                        rows = hg[:, sl, :, :]
                    else:
                        rows = (msg if total > G3 + 1 else msg3)[:, sl % 2, :, 0:total]
                    wait_for(pe, k, "acc_done", it, sl, back=sum_banks(k))
                    if kind == SUM:
                        wait_for(pe, k, "msg_ready", it, sl)
                    for j in range(TG):
                        if kind == FILT and j % 2 == 0:
                            wait_for(pe, k, "msg_ready", it, sl, c=j // 2 + 1)
                        last = MM(sum_at(k, sl), oh[:, sl, j, :], rows[:, j, :],
                                  start=(j == 0), stop=(j == TG - 1))
                    last.then_inc(esem["scattered"], 1)

                def turn_attr(it, sl):
                    wait_for(pe, k, "attr_step", it, sl)
                    wait_for(pe, k, "turn_copied", it, sl, back=1)
                    for j in range(TG):
                        last = MM(ps[4][0:RK, j * LANES:(j + 1) * LANES],
                                  apart[:, sl % 2, j, :, :].rearrange("p q c -> p (q c)"), idnb[:, :],
                                  start=True, stop=True)
                    last.then_inc(esem["turned"], 1)

                def hidden(it, sl):
                    wait_for(pe, k, "turn_copied", it, sl)
                    wait_for(pe, k, "hidden_act", it, sl, back=1)
                    for c in range(2):
                        last = MM(ps[5 + c][:, :], wf1k[:, c * LANES:(c + 1) * LANES], rT[:, sl % 2, :],
                                  start=True, stop=True)
                    last.then_inc(esem["hidden"], 1)

                def filt(it, sl):
                    wait_for(pe, k, "hidden_act", it, sl)
                    for half in range(2):
                        wait_for(pe, k, "msg_ready", it, sl, c=half + 1, back=1)
                        for j in (2 * half, 2 * half + 1):
                            to = ps[2 + half][:, D * (j % 2):D * (j % 2 + 1)]
                            for c in range(2):
                                MM(to, hidT[:, sl % 2, c, j * LANES:(j + 1) * LANES], wf2[:, c, :],
                                   start=(c == 0), stop=False)
                            last = MM(to, ones3[:, :], bf2p[:, :], start=False, stop=True)
                        last.then_inc(esem["filtered"], 1)

                if kind == FILT:
                    pe.wait_ge(s["parts_in"], 16 * (3 + len(W_PART)))
                skewed(pe, NI, SLOTS,
                       {MAX: [(maxima, 0)], MAX1: [(maxima, 0)], WSUM: [(sums, 0)],
                        SUM: [(dst_terms, 1), (turn_onehot, 0), (sums, 2)],
                        FILT: [(filt, 2), (hidden, 1), (sums, 3), (turn_attr, 0)]}[kind])

            edges(0)
            edges(1)
            edges(2)

            def mlp(name, got, freed_by, weight, source, to):
                def stage_(it, sl):
                    nwait(pe, got, it, sl)
                    nwait(pe, freed_by, it, sl, back=2)
                    for m in range(2):
                        for c in range(2):
                            last = MM(to(sl)[:, m * P:(m + 1) * P], weight[:, c, m * LANES:(m + 1) * LANES],
                                      source[:, sl, c, :], start=(c == 0), stop=(c == 1))
                    last.then_inc(nsem(name), 1)
                return stage_

            def turn_back(name, got, freed_by, at):
                def stage_(it, sl):
                    nwait(pe, got, it, sl)
                    nwait(pe, freed_by[0], it, sl, back=freed_by[1])
                    for c in range(2):
                        last = nc.tensor.transpose(at(sl)[0:P, c * LANES:(c + 1) * LANES], tT[:, sl, c, :],
                                                   idn[:, :])
                    last.then_inc(nsem(name), 1)
                return stage_
            tiles(pe, (turn("t2", "a2", "c2", banks=2), 0), (mlp("p2", "c2", "b2", wu1, tT, second_at), 1),
                  (mlp("q2", "b2", "y2", wu2, gu, third_at), 2))
            tiles(pe, (turn_back("g2", "h2", ("e2", NSL), lambda sl: ps[3 + sl]), 0))

            tiles(pe, (turn("t3", "a3", "c3"), 0))
            tiles(pe, (table("m3", "h3", "f3", wio, 2 * D), 0))
            edges(3)
            edges(4)

            def turn4(it, sl):
                nwait(pe, "i4", it, sl)
                pe.wait_ge(nsem(f"ld4_{sl}"), 16 * (it + 1))
                nwait(pe, "c4", it, sl, back=1)
                for c in range(4):
                    last = nc.tensor.transpose(ps[0][:, c * P:(c + 1) * P],
                                               (ai if c < 2 else hs)[:, sl, (c % 2) * LANES:(c % 2 + 1) * LANES],
                                               idn[0:P, 0:P])
                last.then_inc(nsem("t4"), 1)

            def gates(it, sl):
                nwait(pe, "c4", it, sl)
                nwait(pe, "g4", it, sl, back=NSL)
                for m in range(4):
                    cut = slice(m * LANES, (m + 1) * LANES)
                    for c in range(4):
                        MM(ps[3 + sl][:, m * P:(m + 1) * P], w_x2i[:, c, cut], aT[:, A_BUF[sl], c, :],
                           start=(c == 0), stop=False)
                    for c in range(2):
                        last = MM(ps[3 + sl][:, m * P:(m + 1) * P], w_h2h[:, c, cut],
                                  r0T[:, c, rows_of(tile_no(it, sl))], start=False, stop=(c == 1))
                last.then_inc(nsem("x4"), 1)
            pe.wait_ge(s["w_late"], 32)
            tiles(pe, (turn4, 0), (gates, 1), (turn_back("z4", "d4", ("y4", 1), lambda sl: ps[1]), 2))

            def first3(it, sl):
                nwait(pe, "c5", it, sl)
                nwait(pe, "b5", it, sl, back=2)
                nwait(pe, "g5", it, sl, back=2)
                for c in range(2):
                    MM(second_at(sl)[0:P, 0:G3 + 2], tT[:, sl, c, :], wg1[:, c, :], start=(c == 0), stop=(c == 1))
                for c in range(2):
                    last = MM(third_at(sl)[0:HID, 0:P], wm1[:, c, :], tT[:, sl, c, :],
                              start=(c == 0), stop=(c == 1))
                last.then_inc(nsem("m5"), 1)
            tiles(pe, (turn("t5", "a5", "c5", banks=2), 0), (first3, 1))

            def mlp3(name, freed_by, weight, source):
                def stage_(it, sl):
                    nwait(pe, freed_by, it, sl, back=NSL)
                    MM(ps[sl][:, 0:P], weight[:, :], source[:, rows_of(tile_no(it, sl))],
                       start=True, stop=True).then_inc(nsem(name), 1)
                return stage_
            wait_once(pe, "relu", "r5")
            tiles(pe, (mlp3("m6", "b6", wm2, m1T), 0))
            wait_once(pe, "relu", "r6")
            tiles(pe, (mlp3("m7", "b7", wm3, m2T), 0))
            all_tiles(pe, "j7")
            edges(5)
            edges(6)

            def table2(it, sl):
                nwait(pe, "c8", it, sl)
                nwait(pe, "o8", it, sl, back=NSL)
                MM(ps[3 + sl][0:P, 0:G3 + 2], tT[0:G3, sl, 0, :], wg2[:, :], start=True, stop=True)\
                    .then_inc(nsem("m8"), 1)
            tiles(pe, (turn("t8", "q8", "c8", G3), 0), (table2, 1))
            edges(7)
            edges(8)

            def latent(it, sl):
                nwait(pe, "c9", it, sl)
                nwait(pe, "w9", it, sl, back=NSL)
                MM(ps[3 + sl][:, 256:256 + P], wgf[:, :], tT[0:G3, sl, 0, :], start=True, stop=True)\
                    .then_inc(nsem("m9"), 1)

            def last3(it, sl):
                nwait(pe, "f9", it, sl)
                MM(ps[3 + sl][0:P, 0:D], onT[:, sl, :], wf[:, :], start=True, stop=True).then_inc(nsem("o9"), 1)
            tiles(pe, (turn("t9", "q9", "c9", G3), 0), (latent, 1), (last3, 2))

        @block.vector
        def _(dve):
            V = nc.vector
            links = [0]

            def link(ins):
                links[0] += 1
                ins.then_inc(s["link"], 1)
                dve.wait_ge(s["link"], links[0])

            V.memset(ones3[:, :], 1.0)
            V.memset(wm2[:, HID:], 0.0)
            V.memset(wm3[:, LAT:], 0.0)
            V.memset(wgf[:, LAT:], 0.0)
            V.memset(onT[LAT:LAT + 1, :, :], 1.0)
            dve.wait_ge(s["consts"], 3)
            V.tensor_copy(iota[:, :], iota_i[:, :])
            V.tensor_copy(group_f, group_i)
            V.tensor_copy(idnb[:, :], idn[:, :])
            link(V.tensor_scalar(idn4[:, :, :], idn[:, :].unsqueeze(1).to_broadcast([LANES, HEADS, LANES]),
                                 -BIG, None, ALU.mult))

            dve.wait_ge(s["in_edges"], 64)
            V.tensor_copy(n_d, ints)
            link(V.tensor_copy(n_s, ints2))

            def split(n, high, low):
                link(V.tensor_scalar(ints, n, 1.0 / P, None, ALU.mult))
                link(V.tensor_copy(high, ints))
                for op, add in ((ALU.is_ge, ALU.add), (ALU.is_lt, ALU.subtract)):
                    link(V.scalar_tensor_tensor(low, high, -float(P), n, ALU.mult, ALU.add))
                    link(V.tensor_scalar(adj, low, float(P) if op == ALU.is_ge else 0.0, None, op))
                    link(V.tensor_tensor(high, high, adj, add))
                link(V.scalar_tensor_tensor(low, high, -float(P), n, ALU.mult, ALU.add))

            def at(order_aux, c):
                return order_aux[:, :, c]

            split(n_d, hi["d"], lo)
            V.tensor_copy(at(aux_d, D_IDX), n_s)
            V.tensor_copy(at(aux_d, D_LO), lo)
            V.tensor_copy(at(aux_d, D_W), ew)
            link(V.memset(at(aux_d, 3), 0.0))
            split(n_s, hi["s"], lo)
            V.memset(at(aux_s, 0), 1.0)
            V.tensor_copy(at(aux_s, S_IDX - RB), n_d)
            V.tensor_copy(at(aux_s, S_LO - RB), lo)
            link(V.tensor_copy(at(aux_s, S_W - RB), ew2))

            steps = [0]

            def chain(ins, per, i, c):
                ins.then_inc(s["sort_step"], 1)
                dve.wait_ge(s["sort_step"], steps[0] + per * i + c)

            def sort(order, n):
                h = hi[order]
                with dve.Fori(0, NNI) as it:
                    for b in (NSL * it + n_ for n_ in range(NSL)):
                        chain(V.tensor_scalar(mask, h, iota[0:P, bass.ds(b, 1)], None, ALU.is_equal), 2, b, 1)
                        chain(V.tensor_reduce(cnt[:, bass.ds(b, 1)], mask, AX, ALU.add), 2, b, 2)
                steps[0] += 2 * NT
                dve.sem_inc(s["cnt_ready"], 1)
                dve.wait_ge(s["prefix_ready"], n)
                link(V.tensor_scalar(tot_i[:, :], ps[0][:, 64:64 + NT], float(GE - 1), None, ALU.add))
                link(V.tensor_scalar(til_i[:, :], tot_i[:, :], GE.bit_length() - 1, None, ALU.logical_shift_right))
                link(V.tensor_copy(til[:, :], til_i[:, :]))
                link(V.tensor_tensor_scan(ends[:, :], til[:, :], til[:, :], 0.0, ALU.add, ALU.bypass))
                link(V.tensor_tensor(start[:, :], ends[:, :], til[:, :], ALU.subtract))
                link(V.scalar_tensor_tensor(base[:, :], start[0:P, :], float(GE), ps[0][0:P, 0:NT],
                                            ALU.mult, ALU.add))
                with dve.Fori(0, NNI) as it:
                    for b in (NSL * it + n_ for n_ in range(NSL)):
                        chain(V.tensor_scalar(mask, h, iota[0:P, bass.ds(b, 1)], None, ALU.is_equal), 3, b, 1)
                        chain(V.tensor_tensor_scan(scan, mask, mask, base[:, bass.ds(b, 1)], ALU.add, ALU.bypass),
                              3, b, 2)
                        dve.sem_inc(s["sort_go"], 1)
                        chain(V.copy_predicated(rank, mask.bitcast(I32), scan), 3, b, 3)
                steps[0] += 3 * NT
                link(V.tensor_scalar(ints, rank, -1.0, None, ALU.add))
                link(V.tensor_scalar(ints2, ints, LANES - 1, None, ALU.bitwise_and))
                link(V.tensor_copy(scan, ints2))
                link(V.tensor_scalar(ints2, ints, 7, None, ALU.logical_shift_right))
                link(V.tensor_copy(rank, ints2))
                V.scalar_tensor_tensor(pos[order], scan, float(T), rank, ALU.mult, ALU.add)\
                    .then_inc(s["sorted_" + order], 1)
                dve.wait_ge(s["sorted_" + order], 1)
                link(V.memset(bsum, 0.0))
                with dve.Fori(1, NT) as b:
                    chain(V.scalar_tensor_tensor(bsum, group_f, start[0:1, bass.ds(b, 1)], bsum,
                                                 ALU.is_ge, ALU.add), 1, b, 0)
                steps[0] += NT - 1
                link(V.tensor_copy(bkt[order][:, :], bsum))

            sort("d", 1)
            sort("s", 2)

            dve.wait_ge(s["w_small"], 16 * len(W_LOADS))
            for c in range(2):
                for n in range(2):
                    link(V.tensor_tensor(wtmp, wx0[:, c, 0:D], att[:, n, :], ALU.mult))
                    link(V.tensor_reduce(wx0[:, c, D + HEADS * n:D + HEADS * (n + 1)],
                                         wtmp.rearrange("p (h f) -> p h f", h=HEADS), AX, ALU.add))
                    link(V.tensor_tensor(wtmp[:, 0:G3], wg1[:, c, 0:G3], att3[:, n, :], ALU.mult))
                    link(V.tensor_reduce(wg1[:, c, G3 + n:G3 + n + 1], wtmp[:, 0:G3], AX, ALU.add))
            for n in range(2):
                link(V.tensor_tensor(wtmp[0:G3, 0:G3], wg2[:, 0:G3], att3[0:G3, 2 + n, :], ALU.mult))
                link(V.tensor_reduce(wg2[:, G3 + n:G3 + n + 1], wtmp[0:G3, 0:G3], AX, ALU.add))
            for whole, rest, part in ((brow[:, 0, :], brow[:, 1, :], bparts), (wf1[:, 0, :], wf1[:, 1, :], wf1p)):
                link(V.tensor_copy(part[:, 0, :], whole))
                link(V.tensor_tensor(rest, whole, part[:, 0, :], ALU.subtract))
                link(V.tensor_copy(part[:, 1, :], rest))
                link(V.tensor_tensor(part[:, 2, :], rest, part[:, 1, :], ALU.subtract))
            dve.sem_inc(s["att_ready"], 1)

            def row_stats(got=None):
                def stage_(it, sl):
                    if got:
                        nwait(dve, got, it, sl)
                    i = tile_no(it, sl)
                    V.bn_stats(flat(lst[:, bass.ds(i, 1), :]), flat(xs[:, bass.ds(i, 1), :])).then_inc(s["ln_stats"], 1)
                return stage_

            def layernorm(n):
                dve.wait_ge(s["ln_stats"], NT * (n + 1))
                even, odd = lst[:, :, 0:3], lst[:, :, 3:6]
                link(V.tensor_tensor(lmean[:, :], even[:, :, 1], odd[:, :, 1], ALU.add))
                link(V.tensor_scalar(lmean[:, :], lmean[:, :], 0.5, None, ALU.mult))
                link(V.tensor_tensor(lrstd[:, :], even[:, :, 1], odd[:, :, 1], ALU.subtract))
                link(V.scalar_tensor_tensor(lrstd[:, :], lrstd[:, :], 0.25, lrstd[:, :], ALU.mult, ALU.mult))
                link(V.tensor_tensor(lvar[:, :], even[:, :, 2], odd[:, :, 2], ALU.add))
                link(V.scalar_tensor_tensor(lvar[:, :], lvar[:, :], 1.0 / D, lrstd[:, :], ALU.mult, ALU.add))
                V.tensor_scalar(lrstd[:, :], lvar[:, :], EPS, None, ALU.add).then_inc(once["variance"], 1)
                wait_once(dve, "deviation", f"ln{n}")
                link(V.reciprocal(lrstd[:, :], lrstd[:, :]))
                V.scalar_tensor_tensor(lnb[:, :], lmean[:, :], -1.0, lrstd[:, :], ALU.mult, ALU.mult)\
                    .then_inc(once["norm"], 1)

            def turn_copy(name, got, freed_by, rows=LANES, chunks=2, banks=3):
                def stage_(it, sl):
                    nwait(dve, got, it, sl)
                    nwait(dve, freed_by, it, sl, back=NSL)
                    V.tensor_copy(tT[0:rows, sl, 0:chunks, :], turned_at(sl, rows, banks)[:, 0:chunks, :])\
                        .then_inc(nsem(name), 1)
                return stage_

            dve.wait_ge(s["in_x"], 16)
            tiles(dve, (row_stats(), 0))
            layernorm(0)
            tiles(dve, (turn_copy("c0", "t0", "m0"), 0))
            all_tiles(dve, "o0")
            V.tensor_copy(adm[:, :, 0:HEADS], tab[:, :, D + HEADS:TABW])
            dve.wait_ge(s["stage_cp"], 2 * NSS)
            V.tensor_copy(acc0[:, :, 0:D], tab[:, :, 0:D])
            V.tensor_copy(mx[:, :, :], tab[:, :, D:D + HEADS])
            V.tensor_copy(own[:, :, :], tab[:, :, D:D + HEADS]).then_inc(once["taken"], 1)
            wait_once(dve, "taken", "h0")

            def bucket(k, it, sl):
                g = SLOTS * it + sl
                return dve.value_load(bkt[PH[k]["order"]][0:1, bass.ds(g, 1)], min_val=0, max_val=NT - 1)

            def edges(k):
                ph = PH[k]
                kind, H, width = ph["kind"], ph.get("heads"), ph["width"]
                dorder = ph["order"] == "d"
                payload, c_lo, c_w = (pay_d, D_LO, D_W) if dorder else (pay_s, S_LO, S_W)
                phase_begins(dve, k)

                def onehots(it, sl):
                    wait_loaded(dve, k, it, sl)
                    wait_for(dve, k, "scattered", it, sl, back=SLOTS)
                    lows = payload[:, sl, :, c_lo:c_lo + 1].to_broadcast([LANES, TG, P])
                    nodes = iota[:, 0:P].unsqueeze(1).to_broadcast([LANES, TG, P])
                    if kind in (MAX, MAX1):
                        last = V.tensor_tensor(ohb[:, sl, :, :], nodes, lows, ALU.not_equal)
                    elif kind == WSUM:
                        for j in range(TG):
                            last = V.tensor_scalar(oh[:, sl, j, :], iota[:, 0:P], payload[:, sl, j, c_lo:c_lo + 1],
                                                   payload[:, sl, j, c_w:c_w + 1], ALU.is_equal, ALU.mult)
                    else:
                        last = V.tensor_tensor(oh[:, sl, :, :], nodes, lows, ALU.is_equal)
                    last.then_inc(esem["onehot"], 1)

                def maxima(it, sl):
                    if kind == MAX:
                        for j in range(TG):
                            wait_for(dve, k, "scattered", it, sl, c=j + 1)
                            V.tensor_reduce(tm[:, sl, j, 0:H], ps[j][0:P, 0:H * LANES]
                                            .rearrange("p (h e) -> p h e", h=H), AX, ALU.max)\
                                .then_inc(esem["reduced"], 1)
                        wait_for(dve, k, "reduced", it, sl, c=TG)
                        V.tensor_reduce(tm2[:, sl, 0:H], tm[:, sl, :, 0:H].rearrange("p j h -> p h j"), AX, ALU.max)\
                            .then_inc(esem["reduced"], 1)
                    else:
                        wait_for(dve, k, "scattered", it, sl)
                        V.tensor_reduce(tm2[:, sl, 0:1], ps[sl][0:P, :], AX, ALU.max).then_inc(esem["reduced"], 1)
                    b = bucket(k, it, sl)
                    wait_for(dve, k, "reduced", it, sl)
                    wait_for(dve, k, "acc_done", it, sl, back=1)
                    m = flat(mx[:, bass.ds(b, 1), 0:H])
                    V.tensor_tensor(m, m, tm2[:, sl, 0:H], ALU.max).then_inc(esem["acc_done"], 1)

                def score0(it, sl):
                    wait_for(dve, k, "dst_terms", it, sl)
                    V.tensor_reduce(term[:, sl % 2, :, 0:2 * H], ps[6 + sl % 2][:, 0:6 * H * TG]
                                    .rearrange("p (j q c) -> p j c q", j=TG, q=3), AX, ALU.add)\
                        .then_inc(esem["score_step"], 1)

                def score1(it, sl):
                    wait_for(dve, k, "score_step", it, sl, c=1)
                    wait_for(dve, k, "exp_ready", it, sl, back=2)
                    span = bass.ds(TG * SLOTS * it + TG * sl, TG)
                    source = as_e[:, span, :] if H == HEADS else keep3[:, span, G3:G3 + 1]
                    V.tensor_tensor(arg[:, sl % 2, :, 0:H], source, term[:, sl % 2, :, 0:H], ALU.add)\
                        .then_inc(esem["score_step"], 1)

                def score2(it, sl):
                    a = arg[:, sl % 2, :, 0:H]
                    wait_for(dve, k, "score_step", it, sl, c=2)
                    V.scalar_tensor_tensor(a, a, SLOPE, a, ALU.mult, ALU.max).then_inc(esem["score_step"], 1)

                def score3(it, sl):
                    a = arg[:, sl % 2, :, 0:H]
                    wait_for(dve, k, "score_step", it, sl, c=3)
                    V.tensor_tensor(a, a, term[:, sl % 2, :, H:2 * H], ALU.min).then_inc(esem["score_step"], 1)

                def score4(it, sl):
                    a = arg[:, sl % 2, :, 0:H]
                    wait_for(dve, k, "score_step", it, sl, c=4)
                    V.tensor_tensor(a, a, term[:, sl % 2, :, H:2 * H], ALU.subtract)\
                        .then_inc(esem["score_step"], 1)

                def attributes(it, sl):
                    whole = pay_s[:, sl, :, 0:RB + 1]
                    part, rest = apart[:, sl % 2, :, :, :], arest[:, sl % 2, :, :]
                    wait_for(dve, k, "turned", it, sl, back=2)
                    V.tensor_copy(part[:, :, 0:3, :], whole.unsqueeze(2).to_broadcast([LANES, TG, 3, RB + 1]))\
                        .then_inc(esem["attr_step"], 1)
                    wait_for(dve, k, "attr_step", it, sl, c=1)
                    V.tensor_tensor(rest, whole, part[:, :, 0, :], ALU.subtract).then_inc(esem["attr_step"], 1)
                    wait_for(dve, k, "attr_step", it, sl, c=2)
                    V.tensor_copy(part[:, :, 3:5, :], rest.unsqueeze(2).to_broadcast([LANES, TG, 2, RB + 1]))\
                        .then_inc(esem["attr_step"], 1)
                    wait_for(dve, k, "attr_step", it, sl, c=3)
                    V.tensor_tensor(part[:, :, 5, :], rest, part[:, :, 3, :], ALU.subtract)\
                        .then_inc(esem["attr_step"], 1)

                def messages(it, sl):
                    if kind == SUM:
                        wait_for(dve, k, "exp_ready", it, sl)
                        wait_for(dve, k, "scattered", it, sl, back=2)
                        if H == HEADS:
                            wait_gathered(dve, k, it, sl)
                            for j in range(TG):
                                last = V.tensor_tensor(
                                    msg[:, sl % 2, j, 0:D].rearrange("p (h f) -> p h f", h=H),
                                    hg[:, sl, j, :].rearrange("p (h f) -> p h f", h=H),
                                    msg[:, sl % 2, j, D:D + H].unsqueeze(2).to_broadcast([LANES, H, FH]), ALU.mult)
                        else:
                            last = V.tensor_tensor(
                                msg3[:, sl % 2, :, 0:G3], keep3[:, bass.ds(TG * SLOTS * it + TG * sl, TG), 0:G3],
                                msg3[:, sl % 2, :, G3:G3 + 1].to_broadcast([LANES, TG, G3]), ALU.mult)
                        last.then_inc(esem["msg_ready"], 1)
                        return
                    wait_gathered(dve, k, it, sl)
                    wait_for(dve, k, "scattered", it, sl, back=2)
                    for half in range(2):
                        wait_for(dve, k, "filtered", it, sl, c=half + 1)
                        V.tensor_tensor(msg[:, sl % 2, 2 * half:2 * half + 2, 0:D],
                                        ps[2 + half][:, :].rearrange("p (j f) -> p j f", j=2),
                                        hg[:, sl, 2 * half:2 * half + 2, :], ALU.mult)\
                            .then_inc(esem["msg_ready"], 1)

                def adds(it, sl):
                    b = bucket(k, it, sl)
                    wait_for(dve, k, "scattered", it, sl)
                    wait_for(dve, k, "acc_done", it, sl, back=1)
                    a = flat(ph["acc"][:, bass.ds(b, 1), :])
                    V.tensor_tensor(a, a, sum_at(k, sl), ALU.add).then_inc(esem["acc_done"], 1)

                skewed(dve, NI, SLOTS,
                       {MAX: [(onehots, 0), (maxima, 1)], MAX1: [(onehots, 0), (maxima, 1)],
                        WSUM: [(onehots, 0), (adds, 2)],
                        SUM: [(onehots, 0), (score0, 1), (messages, 2), (score1, 1), (score2, 1)]
                        + ([(adds, 3)] if ph["table"] is not None else [])
                        + [(score3, 1), (score4, 1)],
                        FILT: [(onehots, 0), (attributes, 0), (messages, 2), (adds, 3)]}[kind])
                dve.wait_ge(esem["acc_done"], before(k + 1, "acc_done"))

            def bounds(H, name):
                m, a, o = adm[:, :, H:2 * H], adm[:, :, 0:H], own[:, :, 0:H]
                V.tensor_tensor(o, o, a, ALU.add)
                link(V.tensor_tensor(m, mx[:, :, 0:H], a, ALU.add))
                V.scalar_tensor_tensor(o, o, SLOPE, o, ALU.mult, ALU.max)
                link(V.scalar_tensor_tensor(m, m, SLOPE, m, ALU.mult, ALU.max))
                rest = adm_rest[:, :, 0:2 * H]
                part = [admp[:, :, 2 * H * q:2 * H * (q + 1)] for q in range(3)]
                link(V.tensor_copy(part[0], adm[:, :, 0:2 * H]))
                link(V.tensor_tensor(rest, adm[:, :, 0:2 * H], part[0], ALU.subtract))
                link(V.tensor_copy(part[1], rest))
                link(V.tensor_tensor(part[2], rest, part[1], ALU.subtract))
                V.tensor_tensor(o, o, m, ALU.subtract).then_inc(once["maxima"], 1)
                wait_once(dve, "own_weight", name)

            edges(0)
            bounds(HEADS, "adm0")
            for h in range(HEADS):
                rows = acc0[:, :, h * FH:(h + 1) * FH]
                V.tensor_tensor(rows, rows, own[:, :, h:h + 1].to_broadcast([P, NT, FH]), ALU.mult)
            link(V.tensor_copy(acc0[:, :, D:D + HEADS], own[:, :, :]))
            edges(1)
            link(V.reciprocal(den[:, :, :], acc0[:, :, D:D + HEADS]))
            for h in range(HEADS):
                last = V.tensor_tensor(acc0[:, :, h * FH:(h + 1) * FH], acc0[:, :, h * FH:(h + 1) * FH],
                                       den[:, :, h:h + 1].to_broadcast([P, NT, FH]), ALU.mult)
            link(last)
            link(V.tensor_tensor(xs, xs, acc0[:, :, 0:D], ALU.add))
            link(V.tensor_tensor(xs, xs, bias0[:, :].unsqueeze(1).to_broadcast([P, NT, D]), ALU.add))

            tiles(dve, (row_stats(), 0))
            layernorm(1)
            link(V.memset(r0, 0.0))
            all_tiles(dve, "a1")
            V.tensor_tensor(xs, xs, r1, ALU.add).then_inc(once["taken"], 1)
            edges(2)

            def node_stats(name, got, source, rows=LANES, chunks=2):
                def stage_(it, sl):
                    nwait(dve, got, it, sl)
                    i = tile_no(it, sl)
                    for c in range(chunks):
                        frm = source[:, c, rows_of(i)] if chunks == 2 else source[:, rows_of(i)]
                        last = V.bn_stats(flat(st[0:rows, c, bass.ds(i, 1), :]), frm)
                    last.then_inc(nsem(name), 1)
                return stage_

            def batchnorm(n, stats, gamma, beta, rows=LANES, chunks=2):
                all_tiles(dve, stats)
                for c in range(chunks):
                    last = V.bn_aggr(mv[0:rows, c, :], st[0:rows, c, :, :].rearrange("p i f -> p (i f)"))
                link(last)
                sc, sh = bsc[0:rows, 0:chunks], bsh[0:rows, 0:chunks]
                V.tensor_scalar(sc, mv[0:rows, 0:chunks, 1], EPS, None, ALU.add).then_inc(once["variance"], 1)
                wait_once(dve, "deviation", f"bn{n}")
                link(V.reciprocal(sc, sc))
                link(V.tensor_tensor(sc, sc, gamma, ALU.mult))
                link(V.tensor_tensor(sh, mv[0:rows, 0:chunks, 0], sc, ALU.mult))
                V.tensor_tensor(sh, beta, sh, ALU.subtract).then_inc(once["norm"], 1)

            tiles(dve, (turn_copy("c2", "t2", "p2", banks=2), 0), (node_stats("j2", "y2", r1T), 3))
            batchnorm(1, "j2", cols[:, 4:6], cols[:, 6:8])

            def x_add(name, got, at_):
                def stage_(it, sl):
                    nwait(dve, got, it, sl)
                    xt = flat(xs[:, bass.ds(tile_no(it, sl), 1), :])
                    V.tensor_tensor(xt, xt, at_(sl)[0:P, 0:D], ALU.add).then_inc(nsem(name), 1)
                return stage_
            tiles(dve, (x_add("e2", "g2", lambda sl: ps[3 + sl]), 0), (row_stats("e2"), 1))

            layernorm(2)

            def feat_T(it, sl):
                nwait(dve, "t3", it, sl)
                V.tensor_copy(r0T[:, :, rows_of(tile_no(it, sl))], turned_at(sl)).then_inc(nsem("c3"), 1)
            tiles(dve, (feat_T, 0), (node_stats("j3", "c3", r0T), 1))
            batchnorm(2, "j3", cols[:, 8:10], cols[:, 10:12])

            def normed_back(it, sl):
                nwait(dve, "h3", it, sl)
                V.tensor_copy(r0T[:, :, rows_of(tile_no(it, sl))], tT[:, sl, :, :]).then_inc(nsem("v3"), 1)

            def feat_bias(it, sl):
                nwait(dve, "m3", it, sl)
                if not first(it):
                    dve.wait_ge(nsem(f"k3_{sl}"), 32 * it)
                V.tensor_tensor(fio[:, sl, :], ps[3 + sl][0:P, :], bias_io[:, :], ALU.add).then_inc(nsem("f3"), 1)
            tiles(dve, (normed_back, 0), (feat_bias, 1))
            link(V.memset(r1, 0.0))
            edges(3)
            dve.wait_ge(s["spill"], 16)
            link(V.memset(r1, 0.0))
            edges(4)

            def blend(it, sl):
                nwait(dve, "g4", it, sl)
                nwait(dve, "z4", it, sl, back=NSL)
                ig, ng, o = gT[:, 0:2, :], gT[:, 2:4, :], tT[:, sl, :, :]
                h_ = r0T[:, :, rows_of(tile_no(it, sl))]
                for c, (a, b, op) in enumerate(((h_, ng, ALU.subtract), (o, ig, ALU.mult), (o, ng, ALU.add))):
                    if c:
                        nwait(dve, "d4", it, sl, c=c)
                    ins = V.tensor_tensor(o, a, b, op).then_inc(nsem("d4"), 1)
            tiles(dve, (blend, 0), (x_add("y4", "z4", lambda sl: ps[1]), 1), (row_stats("y4"), 2))

            layernorm(3)

            def table3(name, got, at_):
                def stage_(it, sl):
                    nwait(dve, got, it, sl)
                    V.tensor_copy(flat(tb3[:, bass.ds(tile_no(it, sl), 1), :]), at_(sl)[0:P, 0:G3 + 2])\
                        .then_inc(nsem(name), 1)
                return stage_
            tiles(dve, (turn_copy("c5", "t5", "m5", banks=2), 0), (table3("g5", "m5", second_at), 2),
                  (node_stats("j5", "b5", m1T, HID, 1), 3))
            batchnorm(5, "j5", cols3[:, 1:2], cols3[:, 2:3], HID, 1)
            tiles(dve, (node_stats("j6", "b6", m2T, HID, 1), 0))
            batchnorm(6, "j6", cols3[:, 4:5], cols3[:, 5:6], HID, 1)
            tiles(dve, (node_stats("j7", "b7", latT, LAT, 1), 0))
            batchnorm(7, "j7", cols3[0:LAT, 7:8], cols3[0:LAT, 8:9], LAT, 1)

            def attention(k, n):
                link(V.tensor_copy(adm[:, :, 0:1], tb3[:, :, G3 + 1:G3 + 2]))
                V.tensor_copy(mx[:, :, 0:1], tb3[:, :, G3:G3 + 1])
                link(V.tensor_copy(own[:, :, 0:1], tb3[:, :, G3:G3 + 1]))
                edges(k)
                bounds(1, f"adm{k}")
                V.tensor_copy(acc3[:, :, G3:G3 + 1], own[:, :, 0:1])
                link(V.tensor_tensor(acc3[:, :, 0:G3], tb3[:, :, 0:G3],
                                     own[:, :, 0:1].to_broadcast([P, NT, G3]), ALU.mult))
                dve.sem_inc(once["sums_begun"], 1)
                edges(k + 1)
                link(V.reciprocal(den[:, :, 0:1], acc3[:, :, G3:G3 + 1]))
                rows = acc3[:, :, 0:G3]
                link(V.tensor_tensor(rows, rows, den[:, :, 0:1].to_broadcast([P, NT, G3]), ALU.mult))
                V.tensor_tensor(rows, rows, bg[:, n, :].unsqueeze(1).to_broadcast([P, NT, G3]), ALU.add)\
                    .then_inc(once["attended"], 1)

            attention(5, 0)
            tiles(dve, (turn_copy("c8", "t8", "m8", G3, 1), 0), (table3("o8", "m8", lambda sl: ps[3 + sl]), 1))
            all_tiles(dve, "o8")
            attention(7, 1)

            def blend3(it, sl):
                nwait(dve, "b9", it, sl)
                nwait(dve, "o9", it, sl, back=NSL)
                V.tensor_scalar(tT[0:LAT, sl, 1, :], tT[0:LAT, sl, 1, :], 0.5, None, ALU.mult)\
                    .then_inc(nsem("f9"), 1)
                nwait(dve, "f9", it, sl, c=1)
                V.scalar_tensor_tensor(onT[0:LAT, sl, :], latT[:, rows_of(tile_no(it, sl))], 0.5,
                                       tT[0:LAT, sl, 1, :], ALU.mult, ALU.add).then_inc(nsem("f9"), 1)

            def x_out(it, sl):
                nwait(dve, "w9", it, sl)
                dve.wait_ge(nsem(f"ld9_{sl}"), 16 * (it + 1))
                V.tensor_tensor(r1[:, sl, :], r1[:, sl, :], hs[:, sl, :], ALU.add).then_inc(nsem("y9"), 1)
            dve.wait_ge(s["lat_in"], 16)
            tiles(dve, (turn_copy("c9", "t9", "m9", G3, 1), 0), (blend3, 2), (x_out, 3))


_FIRST = ["x", "src", "dst", "edge_attr_20", "edge_weight", "edge_weight_n2"]
_WEIGHTS = (["L0_gnn_" + n for n in ("W", "att_src", "att_dst", "bias")]
            + ["L1_gnn_" + n for n in ("Wf1", "bf1", "Wf2", "bf2", "Wu1", "bu1", "Wu2", "bu2", "gamma", "beta")]
            + ["L2_gnn_" + n for n in ("gamma", "beta", "W_in", "b_in", "W_out", "b_out", "W_x2i", "b_x2i", "W_h2h")]
            + ["L3_gnn_" + n for n in (
                "W_g1", "as_g1", "ad_g1", "b_g1", "W_g2", "as_g2", "ad_g2", "b_g2", "W_gf", "b_gf", "W_m1", "b_m1",
                "g_m1", "be_m1", "W_m2", "b_m2", "g_m2", "be_m2", "W_m3", "b_m3", "g_m3", "be_m3", "W_f", "b_f")])


def kernel(**inputs):
    import numpy as _np
    import concourse.bacc as _bacc
    from concourse import mybir as _mybir
    from concourse.bass_utils import run_bass_kernel_spmd as _run

    nc = _bacc.Bacc("TRN2", target_bir_lowering=False, num_devices=1)
    arrays, aps = {}, {}
    for name in _FIRST + _WEIGHTS:
        a = _np.ascontiguousarray(inputs[name])
        arrays[f"in_{name}"] = a
        aps[name] = nc.dram_tensor(f"in_{name}", a.shape, _mybir.dt.from_np(a.dtype), kind="ExternalInput").ap()
    out = nc.dram_tensor("out_0", (N, D), F32, kind="ExternalOutput").ap()
    gnn_kernel(nc, *(aps[n] for n in _FIRST), {n: aps[n] for n in _WEIGHTS}, out)
    r = _run(nc, [arrays], core_ids=[0])
    return r.results[0]["out_0"]
```
